# Optimizing a Trainium2 kernel written in Bass

```python
import numpy as np
import jax
import jax.numpy as jnp

def _softmax(x, axis=-1):
    return jax.nn.softmax(x, axis=axis)

def _gelu(x):
    return jax.nn.gelu(x, approximate=True)

def _silu(x):
    return jax.nn.silu(x)

def _sigmoid(x):
    return jax.nn.sigmoid(x)

def _layernorm(x, axis=-1, eps=1e-05):
    m = jnp.mean(x, axis=axis, keepdims=True)
    v = jnp.var(x, axis=axis, keepdims=True)
    return (x - m) / jnp.sqrt(v + eps)

def _scatter_add(tgt, idx, src, axis=0):
    return tgt.at[idx].add(src)

def _segment_sum(src, seg, n):
    return jax.ops.segment_sum(src, seg, n)
kernel_name = 'mk_adaln_ffn_d2_seqx_r4_e41d29'

def setup_inputs(seed: int=0):
    np.random.seed(seed)
    _w = jnp.asarray

    def _rec_inputs():
        import jax
        import jax.numpy as jnp
        _rk = jax.random.key(seed)
        x = -0.0003929 + 0.9999 * jax.random.normal(jax.random.fold_in(_rk, 1), (128, 64, 1024), jnp.float32)
        _lenS = 64 - jax.random.randint(jax.random.fold_in(_rk, 7), (128,), 0, max(1, 64 // 4) + 1, jnp.int32)
        _lenS2 = 64 - jax.random.randint(jax.random.fold_in(_rk, 8), (128,), 0, max(1, 64 // 4) + 1, jnp.int32)
        cond_512 = 0.00782532 + 1.00527 * jax.random.normal(jax.random.fold_in(_rk, 11), (128, 128), jnp.float32)
        return (x, cond_512)
    x, cond_512 = _rec_inputs()

    def _L0_cond_setup():
        import jax, jax.numpy as jnp
        from jax import lax
        import numpy as np
        CIN, COUT, K, STYLE_DIM = (64, 64, 3, 128)
        N_LAYERS = 4
        TYPES = ('same', 'upsample', 'same', 'downsample')
        SCALE = 1.0 / float(np.sqrt(CIN * K ** 2))
        EPS = 1e-08
        _BK = np.array([1.0, 3.0, 3.0, 1.0], dtype=np.float32)
        BLUR_K = _BK / _BK.sum()

        def _blur(x, kern, pad):
            B, C, _ = x.shape
            xp = jnp.pad(x, ((0, 0), (0, 0), (pad[0], pad[1])))
            w = jnp.broadcast_to(kern.astype(x.dtype)[None, None, :], (C, 1, kern.shape[0]))
            return lax.conv_general_dilated(xp, w, (1,), 'VALID', feature_group_count=C, dimension_numbers=('NCH', 'OIH', 'NCH'))

        def _conv_same(x, w):
            p = (K - 1) // 2
            return lax.conv_general_dilated(x[None], w, (1,), [(p, p)], dimension_numbers=('NCH', 'OIH', 'NCH'))[0]

        def _conv_down(x, w):
            return lax.conv_general_dilated(x[None], w, (2,), 'VALID', dimension_numbers=('NCH', 'OIH', 'NCH'))[0]

        def _conv_up(x, w_t):
            return lax.conv_transpose(x[None], w_t, (2,), 'VALID', dimension_numbers=('NCH', 'IOH', 'NCH'), transpose_kernel=True)[0]

        def _layer(x, style, w, b, mw, mb, typ):
            s = style @ mw.T + mb
            weight = SCALE * w * s[:, None, :, None]
            demod = lax.rsqrt(jnp.sum(weight * weight, axis=(2, 3)) + EPS)
            weight = weight * demod[:, :, None, None]
            blur_k = jnp.asarray(BLUR_K)
            if typ == 'same':
                out = jax.vmap(_conv_same)(x, weight) + b[None, :, None]
            elif typ == 'upsample':
                out = jax.vmap(_conv_up)(x, weight.transpose(0, 2, 1, 3)) + b[None, :, None]
                out = _blur(out, 2.0 * blur_k, (1, 1))
            elif typ == 'downsample':
                xb = _blur(x, blur_k, (2, 2))
                out = jax.vmap(_conv_down)(xb, weight) + b[None, :, None]
            else:
                raise NotImplementedError(typ)
            return out
        key = jax.random.key(seed)
        ks = jax.random.split(key, 6)
        B, L = (16, 1024)
        return {'x': jax.random.normal(ks[0], (B, CIN, L), dtype=jnp.float32), 'style': jax.random.normal(ks[1], (B, STYLE_DIM), dtype=jnp.float32), 'weights': jax.random.normal(ks[2], (N_LAYERS, COUT, CIN, K), dtype=jnp.float32), 'biases': jax.random.normal(ks[3], (N_LAYERS, COUT), dtype=jnp.float32) * 0.1, 'mod_w': jax.random.normal(ks[4], (N_LAYERS, CIN, STYLE_DIM), dtype=jnp.float32) / np.sqrt(STYLE_DIM), 'mod_b': 1.0 + 0.1 * jax.random.normal(ks[5], (N_LAYERS, CIN), dtype=jnp.float32)}
    _L0_cond_all = _L0_cond_setup()
    _L0_cond_in = {k: v for k, v in _L0_cond_all.items() if k in ('weights', 'biases', 'mod_w', 'mod_b')}
    del _L0_cond_all

    def _L0_ffn_setup():
        import jax, jax.numpy as jnp
        import numpy as np
        LORA_R = 16
        SCALE = 16.0 / np.sqrt(16.0)
        NUM_EXPERTS = 4
        TOP_K = 2
        IN_F = 1024
        OUT_F = 1024
        key = jax.random.key(seed)
        k_x, k_a, k_b, k_r = jax.random.split(key, 4)
        x = jax.random.normal(k_x, (2, 512, IN_F), dtype=jnp.float32)
        A = jax.random.normal(k_a, (NUM_EXPERTS, LORA_R, IN_F), dtype=jnp.float32) * (1.0 / np.sqrt(IN_F))
        B = jax.random.normal(k_b, (NUM_EXPERTS, OUT_F, LORA_R), dtype=jnp.float32) * 0.02
        Wr = jax.random.normal(k_r, (NUM_EXPERTS, IN_F), dtype=jnp.float32) * 0.02
        return {'x': x, 'A': A, 'B': B, 'Wr': Wr}
    _L0_ffn_all = _L0_ffn_setup()
    _L0_ffn_in = {k: v for k, v in _L0_ffn_all.items() if k in ('A', 'B', 'Wr')}
    del _L0_ffn_all

    def _L1_cond_setup():
        import jax, jax.numpy as jnp
        from jax import lax
        import numpy as np
        CIN, COUT, K, STYLE_DIM = (64, 64, 3, 128)
        N_LAYERS = 4
        TYPES = ('same', 'upsample', 'same', 'downsample')
        SCALE = 1.0 / float(np.sqrt(CIN * K ** 2))
        EPS = 1e-08
        _BK = np.array([1.0, 3.0, 3.0, 1.0], dtype=np.float32)
        BLUR_K = _BK / _BK.sum()

        def _blur(x, kern, pad):
            B, C, _ = x.shape
            xp = jnp.pad(x, ((0, 0), (0, 0), (pad[0], pad[1])))
            w = jnp.broadcast_to(kern.astype(x.dtype)[None, None, :], (C, 1, kern.shape[0]))
            return lax.conv_general_dilated(xp, w, (1,), 'VALID', feature_group_count=C, dimension_numbers=('NCH', 'OIH', 'NCH'))

        def _conv_same(x, w):
            p = (K - 1) // 2
            return lax.conv_general_dilated(x[None], w, (1,), [(p, p)], dimension_numbers=('NCH', 'OIH', 'NCH'))[0]

        def _conv_down(x, w):
            return lax.conv_general_dilated(x[None], w, (2,), 'VALID', dimension_numbers=('NCH', 'OIH', 'NCH'))[0]

        def _conv_up(x, w_t):
            return lax.conv_transpose(x[None], w_t, (2,), 'VALID', dimension_numbers=('NCH', 'IOH', 'NCH'), transpose_kernel=True)[0]

        def _layer(x, style, w, b, mw, mb, typ):
            s = style @ mw.T + mb
            weight = SCALE * w * s[:, None, :, None]
            demod = lax.rsqrt(jnp.sum(weight * weight, axis=(2, 3)) + EPS)
            weight = weight * demod[:, :, None, None]
            blur_k = jnp.asarray(BLUR_K)
            if typ == 'same':
                out = jax.vmap(_conv_same)(x, weight) + b[None, :, None]
            elif typ == 'upsample':
                out = jax.vmap(_conv_up)(x, weight.transpose(0, 2, 1, 3)) + b[None, :, None]
                out = _blur(out, 2.0 * blur_k, (1, 1))
            elif typ == 'downsample':
                xb = _blur(x, blur_k, (2, 2))
                out = jax.vmap(_conv_down)(xb, weight) + b[None, :, None]
            else:
                raise NotImplementedError(typ)
            return out
        key = jax.random.key(seed)
        ks = jax.random.split(key, 6)
        B, L = (16, 1024)
        return {'x': jax.random.normal(ks[0], (B, CIN, L), dtype=jnp.float32), 'style': jax.random.normal(ks[1], (B, STYLE_DIM), dtype=jnp.float32), 'weights': jax.random.normal(ks[2], (N_LAYERS, COUT, CIN, K), dtype=jnp.float32), 'biases': jax.random.normal(ks[3], (N_LAYERS, COUT), dtype=jnp.float32) * 0.1, 'mod_w': jax.random.normal(ks[4], (N_LAYERS, CIN, STYLE_DIM), dtype=jnp.float32) / np.sqrt(STYLE_DIM), 'mod_b': 1.0 + 0.1 * jax.random.normal(ks[5], (N_LAYERS, CIN), dtype=jnp.float32)}
    _L1_cond_all = _L1_cond_setup()
    _L1_cond_in = {k: v for k, v in _L1_cond_all.items() if k in ('weights', 'biases', 'mod_w', 'mod_b')}
    del _L1_cond_all

    def _L1_ffn_setup():
        import jax, jax.numpy as jnp
        import numpy as np
        R = 16
        ALPHA = 32
        SCALING = ALPHA / R
        E = 8
        TOP_K = 2
        key = jax.random.key(seed)
        ks = jax.random.split(key, 5)
        B, S, D = (4, 512, 1024)
        x = jax.random.normal(ks[0], (B, S, D), dtype=jnp.float32)
        base_W = jax.random.normal(ks[1], (D, D), dtype=jnp.float32) * 0.02
        router_W = jax.random.normal(ks[2], (E, D), dtype=jnp.float32) * 0.02
        lora_A = jax.random.normal(ks[3], (E, D, R), dtype=jnp.float32) * 0.02
        lora_B = jax.random.normal(ks[4], (E, R, D), dtype=jnp.float32) * 0.02
        return {'x': x, 'base_W': base_W, 'router_W': router_W, 'lora_A': lora_A, 'lora_B': lora_B}
    _L1_ffn_all = _L1_ffn_setup()
    _L1_ffn_in = {k: v for k, v in _L1_ffn_all.items() if k in ('base_W', 'router_W', 'lora_A', 'lora_B')}
    del _L1_ffn_all
    return {'x': x, 'cond_512': cond_512, 'L0_cond_weights': _L0_cond_in['weights'], 'L0_cond_biases': _L0_cond_in['biases'], 'L0_cond_mod_w': _L0_cond_in['mod_w'], 'L0_cond_mod_b': _L0_cond_in['mod_b'], 'L0_ffn_A': _L0_ffn_in['A'], 'L0_ffn_B': _L0_ffn_in['B'], 'L0_ffn_Wr': _L0_ffn_in['Wr'], 'L1_cond_weights': _L1_cond_in['weights'], 'L1_cond_biases': _L1_cond_in['biases'], 'L1_cond_mod_w': _L1_cond_in['mod_w'], 'L1_cond_mod_b': _L1_cond_in['mod_b'], 'L1_ffn_base_W': _L1_ffn_in['base_W'], 'L1_ffn_router_W': _L1_ffn_in['router_W'], 'L1_ffn_lora_A': _L1_ffn_in['lora_A'], 'L1_ffn_lora_B': _L1_ffn_in['lora_B']}

def reference(x, cond_512, L0_cond_weights, L0_cond_biases, L0_cond_mod_w, L0_cond_mod_b, L0_ffn_A, L0_ffn_B, L0_ffn_Wr, L1_cond_weights, L1_cond_biases, L1_cond_mod_w, L1_cond_mod_b, L1_ffn_base_W, L1_ffn_router_W, L1_ffn_lora_A, L1_ffn_lora_B):
    import jax
    import jax.numpy as jnp

    def _L0_cond_ref(x, style, weights, biases, mod_w, mod_b):
        import jax, jax.numpy as jnp
        from jax import lax
        import numpy as np
        CIN, COUT, K, STYLE_DIM = (64, 64, 3, 128)
        N_LAYERS = 4
        TYPES = ('same', 'upsample', 'same', 'downsample')
        SCALE = 1.0 / float(np.sqrt(CIN * K ** 2))
        EPS = 1e-08
        _BK = np.array([1.0, 3.0, 3.0, 1.0], dtype=np.float32)
        BLUR_K = _BK / _BK.sum()

        def _blur(x, kern, pad):
            B, C, _ = x.shape
            xp = jnp.pad(x, ((0, 0), (0, 0), (pad[0], pad[1])))
            w = jnp.broadcast_to(kern.astype(x.dtype)[None, None, :], (C, 1, kern.shape[0]))
            return lax.conv_general_dilated(xp, w, (1,), 'VALID', feature_group_count=C, dimension_numbers=('NCH', 'OIH', 'NCH'))

        def _conv_same(x, w):
            p = (K - 1) // 2
            return lax.conv_general_dilated(x[None], w, (1,), [(p, p)], dimension_numbers=('NCH', 'OIH', 'NCH'))[0]

        def _conv_down(x, w):
            return lax.conv_general_dilated(x[None], w, (2,), 'VALID', dimension_numbers=('NCH', 'OIH', 'NCH'))[0]

        def _conv_up(x, w_t):
            return lax.conv_transpose(x[None], w_t, (2,), 'VALID', dimension_numbers=('NCH', 'IOH', 'NCH'), transpose_kernel=True)[0]

        def _layer(x, style, w, b, mw, mb, typ):
            s = style @ mw.T + mb
            weight = SCALE * w * s[:, None, :, None]
            demod = lax.rsqrt(jnp.sum(weight * weight, axis=(2, 3)) + EPS)
            weight = weight * demod[:, :, None, None]
            blur_k = jnp.asarray(BLUR_K)
            if typ == 'same':
                out = jax.vmap(_conv_same)(x, weight) + b[None, :, None]
            elif typ == 'upsample':
                out = jax.vmap(_conv_up)(x, weight.transpose(0, 2, 1, 3)) + b[None, :, None]
                out = _blur(out, 2.0 * blur_k, (1, 1))
            elif typ == 'downsample':
                xb = _blur(x, blur_k, (2, 2))
                out = jax.vmap(_conv_down)(xb, weight) + b[None, :, None]
            else:
                raise NotImplementedError(typ)
            return out
        out = x
        for i, typ in enumerate(TYPES):
            out = _layer(out, style, weights[i], biases[i], mod_w[i], mod_b[i], typ)
        return out

    def _L0_ffn_ref(x, A, B, Wr):
        import jax, jax.numpy as jnp
        import numpy as np
        LORA_R = 16
        SCALE = 16.0 / np.sqrt(16.0)
        NUM_EXPERTS = 4
        TOP_K = 2
        IN_F = 1024
        OUT_F = 1024
        orig_shape = x.shape
        flat = x.reshape(-1, orig_shape[-1])
        logits = flat @ Wr.T
        topk_vals, topk_idx = jax.lax.top_k(logits, TOP_K)
        T = flat.shape[0]
        neg_inf = jnp.finfo(logits.dtype).min
        sparse = jnp.full_like(logits, neg_inf)
        rows = jnp.arange(T)[:, None]
        sparse = sparse.at[rows, topk_idx].set(topk_vals)
        gates = jax.nn.softmax(sparse, axis=-1)
        mid = jnp.einsum('tf,erf->ter', flat, A)
        all_deltas = jnp.einsum('ter,eor->teo', mid, B) * SCALE
        delta = jnp.sum(gates[:, :, None] * all_deltas, axis=1)
        return delta.reshape(*orig_shape[:-1], -1)

    def _L1_cond_ref(x, style, weights, biases, mod_w, mod_b):
        import jax, jax.numpy as jnp
        from jax import lax
        import numpy as np
        CIN, COUT, K, STYLE_DIM = (64, 64, 3, 128)
        N_LAYERS = 4
        TYPES = ('same', 'upsample', 'same', 'downsample')
        SCALE = 1.0 / float(np.sqrt(CIN * K ** 2))
        EPS = 1e-08
        _BK = np.array([1.0, 3.0, 3.0, 1.0], dtype=np.float32)
        BLUR_K = _BK / _BK.sum()

        def _blur(x, kern, pad):
            B, C, _ = x.shape
            xp = jnp.pad(x, ((0, 0), (0, 0), (pad[0], pad[1])))
            w = jnp.broadcast_to(kern.astype(x.dtype)[None, None, :], (C, 1, kern.shape[0]))
            return lax.conv_general_dilated(xp, w, (1,), 'VALID', feature_group_count=C, dimension_numbers=('NCH', 'OIH', 'NCH'))

        def _conv_same(x, w):
            p = (K - 1) // 2
            return lax.conv_general_dilated(x[None], w, (1,), [(p, p)], dimension_numbers=('NCH', 'OIH', 'NCH'))[0]

        def _conv_down(x, w):
            return lax.conv_general_dilated(x[None], w, (2,), 'VALID', dimension_numbers=('NCH', 'OIH', 'NCH'))[0]

        def _conv_up(x, w_t):
            return lax.conv_transpose(x[None], w_t, (2,), 'VALID', dimension_numbers=('NCH', 'IOH', 'NCH'), transpose_kernel=True)[0]

        def _layer(x, style, w, b, mw, mb, typ):
            s = style @ mw.T + mb
            weight = SCALE * w * s[:, None, :, None]
            demod = lax.rsqrt(jnp.sum(weight * weight, axis=(2, 3)) + EPS)
            weight = weight * demod[:, :, None, None]
            blur_k = jnp.asarray(BLUR_K)
            if typ == 'same':
                out = jax.vmap(_conv_same)(x, weight) + b[None, :, None]
            elif typ == 'upsample':
                out = jax.vmap(_conv_up)(x, weight.transpose(0, 2, 1, 3)) + b[None, :, None]
                out = _blur(out, 2.0 * blur_k, (1, 1))
            elif typ == 'downsample':
                xb = _blur(x, blur_k, (2, 2))
                out = jax.vmap(_conv_down)(xb, weight) + b[None, :, None]
            else:
                raise NotImplementedError(typ)
            return out
        out = x
        for i, typ in enumerate(TYPES):
            out = _layer(out, style, weights[i], biases[i], mod_w[i], mod_b[i], typ)
        return out

    def _L1_ffn_ref(x, base_W, router_W, lora_A, lora_B):
        import jax, jax.numpy as jnp
        import numpy as np
        R = 16
        ALPHA = 32
        SCALING = ALPHA / R
        E = 8
        TOP_K = 2
        base = jnp.einsum('bsd,od->bso', x, base_W)
        logits = jnp.einsum('bsd,ed->bse', x, router_W)
        probs = jax.nn.softmax(logits.astype(jnp.float32), axis=-1)
        top_vals, top_idx = jax.lax.top_k(probs, TOP_K)
        rw = top_vals / jnp.sum(top_vals, axis=-1, keepdims=True)
        w_dense = jnp.sum(jax.nn.one_hot(top_idx, E, dtype=rw.dtype) * rw[..., None], axis=-2).astype(x.dtype)
        mid = jnp.einsum('bsd,edr->bser', x, lora_A)
        mid = mid * w_dense[..., None]
        inc = jnp.einsum('bser,erd->bsd', mid, lora_B)
        return base + inc * SCALING
    x = x + _L0_ffn_ref(_L0_cond_ref(x, cond_512, L0_cond_weights, L0_cond_biases, L0_cond_mod_w, L0_cond_mod_b), L0_ffn_A, L0_ffn_B, L0_ffn_Wr)
    x = x + _L1_ffn_ref(_L1_cond_ref(x, cond_512, L1_cond_weights, L1_cond_biases, L1_cond_mod_w, L1_cond_mod_b), L1_ffn_base_W, L1_ffn_router_W, L1_ffn_lora_A, L1_ffn_lora_B)
    return x

_drawn_inputs = setup_inputs


def setup_inputs(seed=0):
    import zlib

    import numpy as np

    out = dict(_drawn_inputs(seed))
    spreads = {}
    factors = {}
    for name, (base, spread) in spreads.items():
        noise = np.random.default_rng([zlib.crc32(name.encode()), seed]).standard_normal(out[name].shape)
        drawn = base * np.exp(spread * noise) if base else spread * noise
        out[name] = jnp.asarray(drawn.astype(out[name].dtype))
    for name, factor in factors.items():
        out[name] = (out[name] * factor).astype(out[name].dtype)
    return out
```

```python
from contextlib import ExitStack

import concourse.bass as bass
from concourse import mybir

F32 = mybir.dt.float32
F32R = mybir.dt.float32r
ALU = mybir.AluOpType
ACT = mybir.ActivationFunctionType
AX_X = mybir.AxisListType.X

P = 128
HALF = 64
PAD_LOGIT = -3.0e38


def build(nc, x, cond, conv_w, conv_b, mod_w, mod_b, A0, B0, Wr0, baseW, routW, A1, B1, out):
    B, C, L = x.shape
    K = 3
    NL = 4
    NPAIR = B // 2
    H = L // 2
    SCALE = 1.0 / float((C * K ** 2) ** 0.5)
    EPS = 1e-8
    E0, R = A0.shape[0], A0.shape[1]
    E1 = A1.shape[0]
    N0 = E0 * R
    N1 = E1 * R
    PROJ0 = N0 + E0
    MIDS1 = N1 + E1
    WC = L + MIDS1
    KT = L // P
    IB = KT // 2
    LORA0_SCALE = 16.0 / 4.0
    LORA1_SCALE = 32.0 / 16.0
    assert C == HALF and K == 3 and L == 1024 and N0 == 64 and N1 == 128 and B % 2 == 0 and NPAIR >= 3

    x_rows = x.rearrange("b c t -> (b c) t")
    out_rows = out.rearrange("b c t -> (b c) t")

    with ExitStack() as ctx:
        def sb(name, shape, dt=F32):
            return ctx.enter_context(nc.sbuf_tensor(name, shape, dt))

        def psum(name, shape):
            return ctx.enter_context(nc.psum_tensor(name, shape, F32))

        def sem(name):
            return ctx.enter_context(nc.semaphore(name))

        def sem_gs(name):
            return [[sem(f"{name}_g{g}_s{s}") for s in range(2)] for g in range(2)]

        def sem_gsl(name, layers):
            return [[[sem(f"{name}_g{g}_s{s}_l{l}") for l in range(layers)] for s in range(2)] for g in range(2)]

        TILES = {0: 0, 1: 2, 2: 6, 3: 8}
        NT = 12
        cw = [sb(f"conv_w_{h}", [P, 2, NT, P], F32R) for h in ("hi", "lo")]
        w1 = [sb(f"ffn1_w_{h}", [P, KT, WC], F32R) for h in ("hi", "lo")]
        w0 = [sb(f"ffn0_w_{h}", [P, KT, PROJ0], F32R) for h in ("hi", "lo")]
        b0s = sb("lora_b0_hi_over_lo", [P, L], F32R)
        b1s = [sb(f"lora_b1_{h}", [P, L], F32R) for h in ("hi", "lo")]

        X2 = sb("x_twice", [P, 2, L + 2])
        P0 = [sb(f"p0_{h}", [P, 2, H + 2], F32R) for h in ("hi", "lo")]
        P1 = [sb(f"p1_{h}", [P, 2, H + 2], F32R) for h in ("hi", "lo")]
        P2 = [sb(f"p2_{h}", [P, 2, L + 2], F32R) for h in ("hi", "lo")]
        P3_ODD = H + 3
        P3 = [sb(f"p3_{h}", [P, 2, 2 * P3_ODD], F32R) for h in ("hi", "lo")]
        V = sb("layer_value", [P, 2, L])
        Y = sb("conv_out", [P, 2, H])
        yT = [sb(f"y_t_{h}", [P, KT, P], F32R) for h in ("hi", "lo")]
        XN = sb("x_rows_sb", [P, L])
        X1 = sb("x1_rows", [P, L])
        tab = sb("scales", [P, 2, 8, B])
        T_S0, T_SC0, T_B0, T_SC1, T_B1, T_SC2, T_B2, T_SC3 = range(8)
        act_stage = sb("act_stage", [P, 2, 8, 2])
        pool_stage = sb("pool_stage", [P, 2, 2])
        edge_mask = sb("edge_mask", [P, 2])
        edge_corr = sb("edge_corr", [P, 2, 2, 2])
        bias_nat = sb("conv_bias", [P, 2, NL])
        modb_nat = sb("mod_bias", [P, 2, NL])
        ident = sb("ident", [P, P])
        G = [sb("gated0_twice", [P, 2, N0]), sb("gated1", [P, 1, N1])]
        GT = [[sb(f"gated{g}_t_{h}", [P, P], F32R) for h in ("hi", "lo")] for g in range(2)]
        top_in = [sb(f"top_in{g}", [P, 16]) for g in range(2)]
        top_q = sb("top_replaced", [P, 16])
        top_max = sb("top_max", [P, 8])
        top_two = [sb(f"top_two{g}", [P, 8]) for g in range(2)]
        neg_max = sb("neg_max", [P, 2])
        gate_e = sb("gate_exp", [P, 2, 8])
        gate_m = sb("gate_masked", [P, 8])
        gate_s = sb("gate_sum", [P, 2])
        gate_r = sb("gate_recip", [P, 2])
        gate = sb("gate", [P, 8])
        wait_taker = sb("wait_taker", [P, 1])
        comb = sb("tap_combos", [P, 6, C])
        taps = sb("taps_t", [P, K, C])
        quad = sb("tile_build", [P, 4, P])

        ring = psum("psum_conv", [P, 2, 2, H])
        main = psum("psum_main", [P, 2, H])
        tr = psum("psum_transposed", [P, 4, P])
        small = psum("psum_small", [P, 512])
        SM_P0, SM_GT0, SM_M1, SM_GT1 = 0, 0, 128, 384

        ld_small = sem("ld_small")
        ld_a1 = sem("ld_a1")
        ld_b0 = sem("ld_b0")
        ld_b1 = sem("ld_b1")
        ld_p0 = sem("ld_p0")
        ld_rout = sem("ld_rout")
        ld_w = [sem(f"ld_base_w_{i}") for i in range(2)]
        ident_done = sem("ident_done")
        pads_done = sem("pads_done")
        dve_step = sem("dve_step")
        pool_step = sem("pool_step")
        su_w2 = sem("su_w2_ready")
        su_t1 = sem("su_transposed")
        su_c1 = sem("su_transposed_copied")
        su_s = sem("su_styles")
        su_ss = sem("su_styles_squared")
        su_d = sem("su_demod_sums")
        su_v = sem("su_variance")
        su_q = sem("su_sqrt")
        su_tab = sem("su_tables")
        su_wd = sem("su_taps_twice")
        su_tt = sem("su_taps_transposed")
        su_wt = sem("su_w_transposed")
        su_wh = sem("su_w_hi")
        su_wc = sem("su_w_split")
        setup_done = sem("setup_done")

        x2_loaded = [sem(f"x2_loaded_s{s}") for s in range(2)]
        x1_doubled = [sem(f"x1_doubled_s{s}") for s in range(2)]
        xn_loaded = sem("xn_loaded")
        p0_part = sem_gs("p0_part")
        p0_ready = sem_gs("p0_ready")
        conv_done = sem_gsl("conv_done", 4)
        act_done = sem_gsl("act_done", 4)
        lo_done = sem_gsl("lo_done", 3)
        yt_psum = sem_gs("y_transposed")
        yt_hi = sem_gs("yt_hi")
        yt_lo = sem_gs("yt_lo")
        mids_done = [sem(f"mids_done_g{g}") for g in range(2)]
        negmax_done = [sem(f"negmax_done_g{g}") for g in range(2)]
        exp_done = [sem(f"exp_done_g{g}") for g in range(2)]
        gated_done = [sem(f"gated_done_g{g}") for g in range(2)]
        gt_psum = [sem(f"gt_psum_g{g}") for g in range(2)]
        gt_hi = [sem(f"gt_hi_g{g}") for g in range(2)]
        gt_lo = [sem(f"gt_lo_g{g}") for g in range(2)]
        ffn_done = [sem(f"ffn_done_g{g}") for g in range(2)]
        x1_done = sem("x1_done")
        out_done = sem("out_done")
        out_stored = sem("out_stored")
        stage_done = sem("act_stage_done")
        corr_done = [sem(f"edge_corr_done_g{g}") for g in range(2)]
        edge_done = sem_gs("edge_done")
        gate_step = [sem(f"gate_step_g{g}") for g in range(2)]
        pstage_done = sem("pool_stage_done")

        Vf = V[:, :, :].rearrange("p s n -> p (s n)")
        Yf = Y[:, :, :].rearrange("p s n -> p (s n)")
        X2f = X2[:, :, :].rearrange("p s n -> p (s n)")
        FL = 2 * NL
        wn = Vf[:, 0:FL * C * K].rearrange("p (f c k) -> p f c k", f=FL, k=K)
        wn_flat = Vf[:, 0:FL * C * K]
        wsq = X2f[:, 0:FL * C * K]
        w2 = Yf[:, 0:FL * C].rearrange("p (f c) -> p f c", f=FL)
        cond_t = Yf[:, 512:512 + B]
        cond_n = Yf[0:B, 640:768]
        w2t = X1[:, :].rearrange("p (f c) -> p f c", f=FL)
        mw_n = XN[:, :].rearrange("p (f c) -> p f c", f=FL)
        mw_t = X2f[:, 0:FL * P].rearrange("p (f d c) -> p f d c", f=FL, d=2)
        styles = X2f[:, 1026:1026 + FL * B].rearrange("p (f b) -> p f b", f=FL)
        styles_sq = XN[:, 0:FL * B].rearrange("p (f b) -> p f b", f=FL)
        dem = Yf[:, 0:FL * B].rearrange("p (f b) -> p f b", f=FL)
        wd = X2f[:, 0:K * P].rearrange("p (k d c) -> p k d c", k=K, d=2)
        ring_f = ring[:, :, :, :].rearrange("p s b n -> p (s b n)")
        s_psum = ring_f[:, 0:FL * B].rearrange("p (f b) -> p f b", f=FL)
        d_psum = ring_f[:, 1024:1024 + FL * B].rearrange("p (f b) -> p f b", f=FL)
        mwt_psum = ring_f[:, 0:FL * C].rearrange("p (f c) -> p f c", f=FL)
        w2t_psum = ring_f[0:C, 1024:2048].rearrange("p (f c) -> p f c", f=FL)
        wbuf = [XN, X1]

        UP = {(-1, 0): (0, 1, 3), (0, 0): (3, 3, 1), (1, 0): (1, 0, 0),
              (-1, 1): (0, 0, 1), (0, 1): (1, 3, 3), (1, 1): (3, 1, 0)}
        UP_KEYS = list(UP)
        DOWN = {-2: (1, 0, 0), -1: (3, 1, 0), 0: (3, 3, 1), 1: (1, 3, 3), 2: (0, 1, 3), 3: (0, 0, 1)}
        DOWN_KEYS = list(DOWN)

        def fixed_quads():
            a = {(0, 0): None, (1, 0): 0, (0, 1): 0, (1, 1): 1}
            b = {(0, 0): 1, (1, 0): 2, (0, 1): 2, (1, 1): None}
            return [a, b]

        def up_quads():
            k = UP_KEYS.index
            return [{(0, 0): k((-1, 1)), (0, 1): k((-1, 0)), (1, 0): None, (1, 1): None},
                    {(0, 0): k((1, 1)), (0, 1): k((1, 0)), (1, 0): k((0, 1)), (1, 1): k((0, 0))},
                    {(0, 0): k((0, 1)), (0, 1): k((0, 0)), (1, 0): k((-1, 1)), (1, 1): k((-1, 0))},
                    {(0, 0): None, (0, 1): None, (1, 0): k((1, 1)), (1, 1): k((1, 0))}]

        def down_quads():
            res = []
            for j in range(4):
                d = {}
                for kh in range(2):
                    for mh in range(2):
                        pos = 2 * (j - 1) + (1 - kh)
                        h = pos - 2 * (1 - mh)
                        d[(kh, mh)] = DOWN_KEYS.index(h) if h in DOWN else None
                res.append(d)
            return res

        def n_of(g, it):
            return it + 1 if g == 0 else it

        def wait(eng, s, count):
            if isinstance(count, int) and count <= 0:
                return
            eng.wait_ge(s, count)

        def groups(it):
            if isinstance(it, int) and it == 0:
                return (0,)
            if isinstance(it, int) and it == NPAIR:
                return (1,)
            return (0, 1)

        def iterations(eng, body):
            body(0)
            body(1)
            with eng.Fori(2, NPAIR) as it:
                body(it)
            body(NPAIR)

        ACT_N = (2, 3, 2, 1)
        LO_N = (1, 2, 1)
        GATE_STEPS = (9, 12)
        N_PADS = 19

        def p2_view(h, s, half):
            rows = slice(half * C, half * C + C)
            return P2[h][rows, s, 1 - half:L + 1 - half].rearrange("p (m e) -> p e m", e=2)

        def p3_view(h, s):
            return P3[h][:, s, :].rearrange("p (e j) -> p e j", e=2)[:, :, 0:H]

        def wide_part(j, h):
            src = ring_f[:, (j % 2) * 1024:(j % 2) * 1024 + 1024].rearrange("p (t n) -> p t n", t=KT)
            if j < 8:
                return w1[h][:, :, j * P:(j + 1) * P], src
            if j == 8:
                return w0[h][:, :, :], src[:, :, 0:PROJ0]
            if j == 9:
                return w1[h][:, :, L + N1:WC], src[:, :, 0:E1]
            return b0s[h * N0:(h + 1) * N0, :].rearrange("p (t n) -> p t n", t=KT), src[0:N0, :, :]

        block = ctx.enter_context(nc.Block())

        @block.sync
        def _(sp):
            for half in range(2):
                rows = slice(half * C, half * C + C)
                for f in range(2):
                    sp.dma_start(wn_flat[rows, f * 768:(f + 1) * 768].rearrange("p (l n) -> p l n", l=NL),
                                 conv_w[f].rearrange("l o i k -> o l (i k)")).then_inc(ld_small, 16)
                    sp.dma_start(bias_nat[rows, f, :], conv_b[f]).then_inc(ld_small, 16)
                    sp.dma_start(modb_nat[rows, f, :], mod_b[f]).then_inc(ld_small, 16)
            for f in range(2):
                sp.dma_start(mw_n[0:C, NL * f:NL * f + NL, :], mod_w[f].rearrange("l o s -> o l s")
                             ).then_inc(ld_small, 16)
            sp.dma_start(cond_n, cond).then_inc(ld_small, 16)
            wait(sp, su_tab, 1)
            for j in range(8):
                if j >= 2:
                    sp.wait_ge(su_wt, j - 1)
                sp.dma_start(wbuf[j % 2][:, :], baseW[j * P:(j + 1) * P, :]).then_inc(ld_w[j % 2], 16)
            sp.wait_ge(su_wt, 7)
            sp.dma_start(XN[0:N0, :], A0.rearrange("e r d -> (e r) d")).then_inc(ld_p0, 16)
            sp.dma_start(XN[N0:PROJ0, :], Wr0).then_inc(ld_p0, 16)
            sp.wait_ge(su_wt, 8)
            sp.dma_start(X1[0:E1, :], routW).then_inc(ld_rout, 16)
            sp.wait_ge(su_wt, 9)
            for e in range(E0):
                sp.dma_start(XN[:, 0:8 * N0].rearrange("p (t e r) -> p t e r", t=8, e=E0)[:, :, e, :],
                             B0[e].rearrange("(t p) r -> p t r", p=P)).then_inc(ld_b0, 16)
            sp.wait_ge(su_wt, 10)
            for e in range(E1):
                sp.dma_start(X1[:, :].rearrange("p (e b n) -> p e b n", e=E1, b=IB)[:, e],
                             A1[e].rearrange("(b i h) r -> i b (h r)", b=IB, h=2)).then_inc(ld_a1, 16)
            sp.wait_ge(su_wt, 11)
            sp.dma_start(XN[:, :], B1.rearrange("e r d -> (e r) d")).then_inc(ld_b1, 16)
            sp.wait_ge(setup_done, 1)

            def load_doubled(it):
                for s in range(2):
                    if isinstance(it, int) and it == 1:
                        sp.wait_ge(p0_ready[0][s], 1)
                    else:
                        wait(sp, p0_ready[1][s], it - 1)
                    src = x_rows[bass.ds(it * P + s * C, C), :]
                    sp.dma_start(X2[0:C, s, 1:L + 1], src).then_inc(x2_loaded[s], 16)
                    sp.dma_start(X2[C:P, s, 0:L], src).then_inc(x2_loaded[s], 16)

            load_doubled(0)

            def body(it):
                act = groups(it)
                if 0 in act:
                    wait(sp, x1_done, it * 2)
                    sp.dma_start(XN[:, :], x_rows[bass.ds(it * P, P), :]).then_inc(xn_loaded, 16)
                    if not (isinstance(it, int) and it == NPAIR - 1):
                        load_next(it)
                        for s in range(2):
                            wait(sp, p0_ready[0][s], it + 2)
                if 1 in act:
                    wait(sp, out_done, it)
                    sp.dma_start(out_rows[bass.ds((it - 1) * P, P), :], Yf).then_inc(out_stored, 16)
                if 0 in act:
                    wait(sp, x1_done, it * 2 + 2)
                    for s in range(2):
                        src = X1[s * C:(s + 1) * C, :]
                        sp.dma_start(X2[0:C, s, 1:L + 1], src).then_inc(x1_doubled[s], 16)
                        sp.dma_start(X2[C:P, s, 0:L], src).then_inc(x1_doubled[s], 16)

            def load_next(it):
                load_doubled(it + 1)

            body(0)
            body(1)
            with sp.Fori(2, NPAIR - 1) as it:
                body(it)
            body(NPAIR - 1)
            body(NPAIR)
            sp.wait_ge(out_stored, 16 * NPAIR)

        @block.gpsimd
        def _(pool):
            nc.gpsimd.memset(ident[:, :], 0.0).then_inc(pool_step, 1)
            pool.wait_ge(pool_step, 1)
            nc.gpsimd.affine_select(out=ident[:, :], in_=ident[:, :], compare_op=ALU.not_equal, fill=1.0,
                                    base=0, pattern=[[-1, P]], channel_multiplier=1).then_inc(ident_done, 1)
            pads = [(P1[h][:, :, c:c + 1].bitcast(F32), 0.0) for h in range(2) for c in (0, H + 1)]
            pads += [(P2[h][rows, :, c:c + 1].bitcast(F32), 0.0) for h in range(2)
                     for rows, c in ((slice(0, C), 0), (slice(C, P), L))]
            pads += [(P3[h][:, :, c:c + 1].bitcast(F32), 0.0) for h in range(2) for c in (H, P3_ODD - 1)]
            pads += [(edge_mask[:, :], -0.125)]
            pads += [(top_in[0][:, :], PAD_LOGIT), (top_two[0][:, :], PAD_LOGIT),
                     (top_in[1][:, :], -1.0), (top_two[1][:, :], -1.0)]
            pads += [(edge_mask[0:C, 0:1], 0.0), (edge_mask[C:P, 1:2], 0.0)]
            assert len(pads) == N_PADS
            for n, (ap, value) in enumerate(pads):
                nc.gpsimd.memset(ap, value).then_inc(pads_done, 1)
                pool.wait_ge(pads_done, n + 1)
            pool.wait_ge(setup_done, 1)
            for s in range(2):
                nc.gpsimd.memset(X2[0:C, s, 0:1], 0.0).then_inc(pool_step, 1)
                pool.wait_ge(pool_step, 2 + 2 * s)
                nc.gpsimd.memset(X2[C:P, s, L:L + 1], 0.0).then_inc(pool_step, 1)
                pool.wait_ge(pool_step, 3 + 2 * s)

            def split(g, s, n):
                src = X2[:, s, 0:L + 1:2]
                style = pool_stage[:, g, s:s + 1].broadcast_to([P, H + 1])
                hi = P0[0][:, s, 0:H + 1]
                nc.gpsimd.tensor_tensor(hi, src, style, ALU.mult).then_inc(p0_part[g][s], 1)
                pool.wait_ge(p0_part[g][s], n * 2 - 1)
                nc.gpsimd.tensor_tensor(src, src, style, ALU.mult).then_inc(p0_part[g][s], 1)
                pool.wait_ge(p0_part[g][s], n * 2)
                nc.gpsimd.tensor_tensor(P0[1][:, s, 0:H + 1], src, hi.bitcast(F32), ALU.subtract
                                        ).then_inc(p0_ready[g][s], 1)

            def stage(g, pair, count):
                nc.gpsimd.tensor_copy(pool_stage[:, g, :], tab[:, g, T_S0, bass.ds(pair * 2, 2)]
                                      ).then_inc(pstage_done, 1)
                pool.wait_ge(pstage_done, count)

            def split0(it):
                stage(0, it, 1 if isinstance(it, int) and it == 0 else it * 2)
                for s in range(2):
                    pool.wait_ge(x2_loaded[s], (it + 1) * 32)
                    if isinstance(it, int) and it == 1:
                        pool.wait_ge(conv_done[0][s][0], 1)
                    else:
                        wait(pool, conv_done[1][s][0], it - 1)
                    split(0, s, it + 1)

            def split1(it):
                last = isinstance(it, int) and it == NPAIR
                stage(1, it - 1, it * 2 if last else it * 2 + 1)
                for s in range(2):
                    pool.wait_ge(x1_doubled[s], it * 32)
                    pool.wait_ge(conv_done[0][s][0], NPAIR if last else it + 1)
                    split(1, s, it)

            split0(0)
            split0(1)
            split1(1)
            with pool.Fori(2, NPAIR) as it:
                split0(it)
                split1(it)
            split1(NPAIR)

        @block.scalar
        def _(act):
            act.wait_ge(su_v, 1)
            nc.scalar.activation(dem, dem, ACT.Sqrt).then_inc(su_q, 1)
            for j in range(11):
                act.wait_ge(su_wt, j + 1)
                dst, src = wide_part(j, 0)
                nc.scalar.copy(dst, src).then_inc(su_wh, 1)
            act.wait_ge(setup_done, 1)

            def evacuate(g, l, s, it):
                if g not in groups(it):
                    return
                scale = act_stage[:, g, (T_SC0, T_SC1, T_SC2, T_SC3)[l], s:s + 1]
                bias = act_stage[:, g, (T_B0, T_B1, T_B2)[l], s:s + 1] if l < 3 else bias_nat[:, g, 3:4]
                done = act_done[g][s][l]
                act.wait_ge(conv_done[g][s][l], n_of(g, it))
                if (g, l) == (1, 0) and 0 in groups(it):
                    act.wait_ge(lo_done[0][s][1], (it + 1) * LO_N[1])
                if (g, l) == (0, 2) and 1 in groups(it):
                    act.wait_ge(lo_done[1][s][0], it * LO_N[0])
                if (g, l) == (1, 1) and 0 in groups(it):
                    act.wait_ge(lo_done[0][s][2], (it + 1) * LO_N[2])
                if l == 0:
                    src = ring[:, s, 0, :]
                    nc.scalar.activation(P1[0][:, s, 1:H + 1], src, ACT.Identity, bias=bias, scale=scale
                                         ).then_inc(done, 1)
                    nc.scalar.activation(V[:, s, 0:H], src, ACT.Identity, bias=bias, scale=scale
                                         ).then_inc(done, 1)
                elif l == 1:
                    for half in range(2):
                        rows = slice(half * C, half * C + C)
                        nc.scalar.activation(p2_view(0, s, half), ring[rows, s, :, :], ACT.Identity,
                                             bias=bias[rows, :], scale=scale[rows, :]).then_inc(done, 1)
                    nc.scalar.activation(V[:, s, :].rearrange("p (e m) -> p e m", e=2), ring[:, s, :, :],
                                         ACT.Identity, bias=bias, scale=scale).then_inc(done, 1)
                elif l == 2:
                    src = ring[:, s, :, :].rearrange("p b n -> p (b n)").rearrange("p (j e) -> p e j", e=2)
                    nc.scalar.activation(p3_view(0, s), src, ACT.Identity, bias=bias, scale=scale
                                         ).then_inc(done, 1)
                    nc.scalar.activation(V[:, s, :].rearrange("p (e j) -> p e j", e=2), src, ACT.Identity,
                                         bias=bias, scale=scale).then_inc(done, 1)
                else:
                    if g == 0 or (isinstance(it, int) and it == NPAIR):
                        wait(act, out_stored, (it - 1) * 16)
                    nc.scalar.activation(Y[:, s, :], ring[:, s, 0, :], ACT.Identity, bias=bias, scale=scale
                                         ).then_inc(done, 1)

            def turned_hi(g, s, it):
                if g not in groups(it):
                    return
                act.wait_ge(yt_psum[g][s], n_of(g, it))
                nc.scalar.copy(yT[0][:, :, s * C:(s + 1) * C], tr[:, :, :].rearrange("p b (h c) -> p (b h) c", h=2)
                               ).then_inc(yt_hi[g][s], 1)

            def gate_exp(g, it):
                if g not in groups(it):
                    return
                act.wait_ge(negmax_done[g], n_of(g, it))
                n, src = (E0, small[:, SM_P0 + N0:SM_P0 + PROJ0]) if g == 0 else \
                    (E1, small[:, SM_M1 + N1:SM_M1 + MIDS1])
                nc.scalar.activation(gate_e[:, g, 0:n], src, ACT.Exp, bias=neg_max[:, g:g + 1]
                                     ).then_inc(exp_done[g], 1)

            def gated_hi(g, it):
                if g not in groups(it):
                    return
                act.wait_ge(gt_psum[g], n_of(g, it))
                col = (SM_GT0, SM_GT1)[g]
                nc.scalar.copy(GT[g][0][:, :], small[:, col:col + P]).then_inc(gt_hi[g], 1)

            def body(it):
                on = groups(it)
                first = isinstance(it, int) and it == 0
                for g in on:
                    pair = it if g == 0 else it - 1
                    nc.scalar.copy(act_stage[:, g, :, :], tab[:, g, :, bass.ds(pair * 2, 2)]).then_inc(stage_done, 1)
                count = 1 if first else it * 2 + 1
                if isinstance(it, int) and it == NPAIR:
                    count = it * 2
                act.wait_ge(stage_done, count)
                for g in on:
                    for s in range(2):
                        nc.scalar.activation(edge_corr[:, g, s, :], edge_mask[:, :], ACT.Copy,
                                             scale=act_stage[:, g, T_B1, s:s + 1]).then_inc(corr_done[g], 1)
                for g, l in ((0, 0), (0, 1), (1, 0), (0, 2), (1, 1), (0, 3)):
                    evacuate(g, l, 0, it)
                    evacuate(g, l, 1, it)
                evacuate(1, 2, 0, it)
                turned_hi(0, 0, it)
                evacuate(1, 2, 1, it)
                turned_hi(0, 1, it)
                evacuate(1, 3, 0, it)
                gate_exp(0, it)
                evacuate(1, 3, 1, it)
                turned_hi(1, 0, it)
                gated_hi(0, it)
                turned_hi(1, 1, it)
                gate_exp(1, it)
                gated_hi(1, it)

            iterations(act, body)

        @block.vector
        def _(dve):
            chain = [0]

            def link(ins):
                chain[0] += 1
                ins.then_inc(dve_step, 1)
                dve.wait_ge(dve_step, chain[0])

            dve.wait_ge(ld_small, 16 * (12 + 3))
            link(nc.vector.tensor_tensor(wsq, wn_flat, wn_flat, ALU.mult))
            nc.vector.tensor_reduce(w2, wsq.rearrange("p (f c k) -> p f c k", f=FL, k=K), AX_X, ALU.add
                                    ).then_inc(su_w2, 1)
            dve.wait_ge(su_w2, 1)
            dve.wait_ge(su_t1, 1)
            for d in range(2):
                nc.vector.tensor_copy(mw_t[:, :, d, :], mwt_psum).then_inc(su_c1, 1)
            nc.vector.tensor_copy(cond_t, tr[:, 0, 0:B]).then_inc(su_c1, 1)
            nc.vector.tensor_copy(w2t[0:C], w2t_psum).then_inc(su_c1, 1)
            dve.wait_ge(su_s, 1)
            for f in range(FL):
                nc.vector.tensor_scalar(styles[:, f, :], s_psum[:, f, :], modb_nat[:, f // NL, f % NL:f % NL + 1],
                                        None, ALU.add).then_inc(su_ss, 1)
            dve.wait_ge(su_ss, FL)
            nc.vector.tensor_tensor(styles_sq, styles, styles, ALU.mult).then_inc(su_ss, 1)
            dve.wait_ge(su_d, 1)
            nc.vector.tensor_scalar(dem, d_psum, SCALE * SCALE, EPS, ALU.mult, ALU.add).then_inc(su_v, 1)
            dve.wait_ge(su_q, 1)
            link(nc.vector.reciprocal(dem, dem))
            for f in range(2):
                b = NL * f
                link(nc.vector.tensor_copy(tab[:, f, T_S0, :], styles[:, b, :]))
                for dst, v, w, factor in ((T_SC0, dem[:, b, :], dem[:, b + 1, :], SCALE),
                                          (T_SC1, styles[:, b + 1, :], styles[:, b + 2, :], SCALE),
                                          (T_SC2, dem[:, b + 2, :], styles[:, b + 3, :], SCALE)):
                    link(nc.vector.scalar_tensor_tensor(out=tab[:, f, dst, :], in0=v, scalar=factor, in1=w,
                                                        op0=ALU.mult, op1=ALU.mult))
                for dst, v, l, factor in ((T_B0, dem[:, b + 1, :], 0, 1.0), (T_B1, styles[:, b + 2, :], 1, 2.0),
                                          (T_B2, styles[:, b + 3, :], 2, 1.0)):
                    link(nc.vector.tensor_scalar(tab[:, f, dst, :], v, bias_nat[:, f, l:l + 1], factor,
                                                 ALU.mult, ALU.mult))
                link(nc.vector.tensor_scalar(tab[:, f, T_SC3, :], dem[:, b + 3, :], SCALE, None, ALU.mult))
            nc.vector.memset(top_q[:, :], 0.0).then_inc(su_tab, 1)
            dve.wait_ge(su_tab, 1)

            turned = 0
            for f in range(2):
                for l in range(NL):
                    if l == 1:
                        src = wn[:, NL * f + 1, :, :].rearrange("p c k -> p k c")
                    else:
                        turned += 1
                        for d in range(2):
                            nc.vector.tensor_copy(wd[:, :, d, :],
                                                  wn[:, NL * f + l, :, :].rearrange("p c k -> p k c")
                                                  ).then_inc(su_wd, 1)
                        dve.wait_ge(su_tt, turned)
                        link(nc.vector.tensor_copy(taps[:, :, :], tr[:, 0:K, 0:C]))
                        src = taps[:, :, :]
                    if l in (0, 2):
                        quads = fixed_quads()
                        made = src
                    else:
                        weights, norm = (UP, 0.25) if l == 1 else (DOWN, 0.125)
                        for n, key in enumerate(weights):
                            some = [(k, c * norm) for k, c in enumerate(weights[key]) if c]
                            link(nc.vector.tensor_scalar(comb[:, n, :], src[:, some[0][0], :], some[0][1], None,
                                                         ALU.mult))
                            for k, c in some[1:]:
                                link(nc.vector.scalar_tensor_tensor(out=comb[:, n, :], in0=src[:, k, :], scalar=c,
                                                                    in1=comb[:, n, :], op0=ALU.mult, op1=ALU.add))
                        quads = up_quads() if l == 1 else down_quads()
                        made = comb[:, :, :]
                    for t, tile in enumerate(quads):
                        for (kh, mh), n in tile.items():
                            dst = quad[kh * C:kh * C + C, t, mh * C:mh * C + C]
                            if n is None:
                                link(nc.vector.memset(dst, 0.0))
                            else:
                                link(nc.vector.tensor_copy(dst, made[kh * C:kh * C + C, n, :]))
                    nt = len(quads)
                    hi = cw[0][:, f, TILES[l]:TILES[l] + nt, :]
                    link(nc.vector.tensor_copy(hi, quad[:, 0:nt, :]))
                    link(nc.vector.tensor_tensor(cw[1][:, f, TILES[l]:TILES[l] + nt, :], quad[:, 0:nt, :],
                                                 hi.bitcast(F32), ALU.subtract))

            for j in range(11):
                dve.wait_ge(su_wh, j + 1)
                hi, src = wide_part(j, 0)
                nc.vector.tensor_tensor(wide_part(j, 1)[0], src, hi.bitcast(F32), ALU.subtract).then_inc(su_wc, 1)
            dve.wait_ge(ld_a1, 16 * E1)
            a1_in = X1[:, :].rearrange("p (e b h r) -> p e b h r", e=E1, b=IB, h=2)
            for ib in range(IB):
                for h in range(2):
                    hi, lo = (w1[i][:, 2 * ib + h, L:L + N1].rearrange("p (e r) -> p e r", e=E1) for i in range(2))
                    link(nc.vector.tensor_copy(hi, a1_in[:, :, ib, 1 - h, :]))
                    link(nc.vector.tensor_tensor(lo, a1_in[:, :, ib, 1 - h, :], hi.bitcast(F32), ALU.subtract))
            dve.wait_ge(ld_b1, 16)
            link(nc.vector.tensor_copy(b1s[0][:, :], XN[:, :]))
            link(nc.vector.tensor_tensor(b1s[1][:, :], XN[:, :], b1s[0][:, :].bitcast(F32), ALU.subtract))
            dve.wait_ge(su_wc, 11)
            dve.wait_ge(pads_done, N_PADS)
            nc.vector.memset(top_q[:, :], 0.0).then_inc(setup_done, 1)

            def low_part(g, l, s, it):
                if g not in groups(it):
                    return
                n = n_of(g, it)
                dve.wait_ge(act_done[g][s][l], n * ACT_N[l])
                done = lo_done[g][s][l]
                if l == 0:
                    nc.vector.tensor_tensor(P1[1][:, s, 1:H + 1], V[:, s, 0:H], P1[0][:, s, 1:H + 1].bitcast(F32),
                                            ALU.subtract).then_inc(done, 1)
                elif l == 1:
                    dve.wait_ge(corr_done[g], n * 2)
                    ends = V[:, s, 0:L:L - 1]
                    nc.vector.tensor_tensor(ends, ends, edge_corr[:, g, s, :], ALU.add).then_inc(edge_done[g][s], 1)
                    dve.wait_ge(edge_done[g][s], n * 3 - 2)
                    nc.vector.tensor_copy(P2[0][C:P, s, 0:1], V[C:P, s, 0:1]).then_inc(edge_done[g][s], 1)
                    nc.vector.tensor_copy(P2[0][0:C, s, L:L + 1], V[0:C, s, L - 1:L]).then_inc(edge_done[g][s], 1)
                    dve.wait_ge(edge_done[g][s], n * 3)
                    for half in range(2):
                        rows = slice(half * C, half * C + C)
                        nc.vector.tensor_tensor(p2_view(1, s, half), V[rows, s, :].rearrange("p (e m) -> p e m", e=2),
                                                p2_view(0, s, half).bitcast(F32), ALU.subtract).then_inc(done, 1)
                else:
                    nc.vector.tensor_tensor(p3_view(1, s), V[:, s, :].rearrange("p (e j) -> p e j", e=2),
                                            p3_view(0, s).bitcast(F32), ALU.subtract).then_inc(done, 1)

            def turned_lo(g, s, it):
                if g not in groups(it):
                    return
                dve.wait_ge(yt_hi[g][s], n_of(g, it))
                cols = slice(s * C, (s + 1) * C)
                nc.vector.tensor_tensor(yT[1][:, :, cols], tr[:, :, :].rearrange("p b (h c) -> p (b h) c", h=2),
                                        yT[0][:, :, cols].bitcast(F32), ALU.subtract).then_inc(yt_lo[g][s], 1)

            def gating(g, it):
                if g not in groups(it):
                    return
                n = n_of(g, it)
                count = [0]

                def step(ins):
                    count[0] += 1
                    ins.then_inc(gate_step[g], 1)
                    dve.wait_ge(gate_step[g], (n - 1) * GATE_STEPS[g] + count[0])

                def settle():
                    nc.vector.memset(wait_taker[:, :], 0.0)

                dve.wait_ge(mids_done[g], n)
                col = (SM_P0, SM_M1)[g]
                ne = (E0, E1)[g]
                nm = (N0, N1)[g]
                logits = small[:, col + nm:col + nm + ne]
                e = gate_e[:, g, 0:ne]
                if g == 0:
                    step(nc.vector.tensor_copy(top_in[0][:, 0:ne], logits))
                    settle()
                    step(nc.vector.max(top_max[:, :], top_in[0][:, :]))
                    nc.vector.tensor_scalar(neg_max[:, 0:1], top_max[:, 0:1], -1.0, None, ALU.mult
                                            ).then_inc(negmax_done[0], 1)
                else:
                    step(nc.vector.tensor_reduce(top_max[:, 0:1], logits, AX_X, ALU.max))
                    nc.vector.tensor_scalar(neg_max[:, 1:2], top_max[:, 0:1], -1.0, None, ALU.mult
                                            ).then_inc(negmax_done[1], 1)
                    dve.wait_ge(exp_done[1], n)
                    step(nc.vector.tensor_reduce(gate_s[:, 1:2], e, AX_X, ALU.add))
                    step(nc.vector.reciprocal(gate_r[:, 1:2], gate_s[:, 1:2]))
                    step(nc.vector.tensor_scalar(top_in[1][:, 0:ne], e, gate_r[:, 1:2], None, ALU.mult))
                    settle()
                    step(nc.vector.max(top_max[:, :], top_in[1][:, :]))
                step(nc.vector.tensor_copy(top_two[g][:, 0:2], top_max[:, 0:2]))
                settle()
                step(nc.vector.match_replace(out=top_q[:, :], in_to_replace=top_two[g][:, :],
                                             in_values=top_in[g][:, :], imm_value=3.0e38))
                step(nc.vector.tensor_tensor(gate_m[:, 0:ne], top_q[:, 0:ne], top_in[g][:, 0:ne], ALU.not_equal))
                if g == 0:
                    dve.wait_ge(exp_done[0], n)
                    step(nc.vector.tensor_tensor(gate[:, 0:ne], gate_m[:, 0:ne], e, ALU.mult))
                else:
                    step(nc.vector.tensor_tensor(gate[:, 0:ne], gate_m[:, 0:ne], top_in[1][:, 0:ne], ALU.mult))
                step(nc.vector.tensor_reduce(gate_s[:, g:g + 1], gate[:, 0:ne], AX_X, ALU.add))
                step(nc.vector.reciprocal(gate_r[:, g:g + 1], gate_s[:, g:g + 1]))
                step(nc.vector.tensor_scalar(gate[:, 0:ne], gate[:, 0:ne], gate_r[:, g:g + 1],
                                             (LORA0_SCALE, LORA1_SCALE)[g], ALU.mult, ALU.mult))
                for d in range(2 - g):
                    nc.vector.tensor_tensor(G[g][:, d, :].rearrange("p (e r) -> p e r", e=ne),
                                            small[:, col:col + nm].rearrange("p (e r) -> p e r", e=ne),
                                            gate[:, 0:ne, None].broadcast_to([P, ne, R]), ALU.mult
                                            ).then_inc(gated_done[g], 1)
                assert count[0] == GATE_STEPS[g]

            def gated_lo(g, it):
                if g not in groups(it):
                    return
                dve.wait_ge(gt_hi[g], n_of(g, it))
                col = (SM_GT0, SM_GT1)[g]
                nc.vector.tensor_tensor(GT[g][1][:, :], small[:, col:col + P], GT[g][0][:, :].bitcast(F32),
                                        ALU.subtract).then_inc(gt_lo[g], 1)

            def add_out(it):
                if 1 not in groups(it):
                    return
                dve.wait_ge(ffn_done[1], it)
                nc.vector.tensor_tensor(Y[:, :, :], X1[:, :].rearrange("p (b n) -> p b n", b=2), main[:, :, :],
                                        ALU.add).then_inc(out_done, 1)

            def add_x1(it):
                if 0 not in groups(it):
                    return
                dve.wait_ge(ffn_done[0], it + 1)
                dve.wait_ge(xn_loaded, (it + 1) * 16)
                wait(dve, out_done, it)
                for s in range(2):
                    wait(dve, x1_doubled[s], it * 32)
                for b in range(2):
                    cols = slice(b * H, (b + 1) * H)
                    nc.vector.tensor_tensor(X1[:, cols], XN[:, cols], ring[:, b, 1, :], ALU.add).then_inc(x1_done, 1)

            def body(it):
                for g, l in ((0, 0), (0, 1), (1, 0), (0, 2), (1, 1)):
                    low_part(g, l, 0, it)
                    low_part(g, l, 1, it)
                low_part(1, 2, 0, it)
                turned_lo(0, 0, it)
                low_part(1, 2, 1, it)
                turned_lo(0, 1, it)
                gating(0, it)
                turned_lo(1, 0, it)
                gated_lo(0, it)
                turned_lo(1, 1, it)
                gating(1, it)
                gated_lo(1, it)
                add_out(it)
                add_x1(it)

            iterations(dve, body)

        @block.tensor
        def _(pe):
            pe.wait_ge(ident_done, 1)
            pe.wait_ge(ld_small, 16 * (12 + 3))
            for f in range(FL):
                nc.tensor.transpose(mwt_psum[:, f, :], mw_n[0:C, f, :], ident[0:C, 0:C])
            nc.tensor.transpose(tr[:, 0, 0:B], cond_n, ident[0:B, 0:B])
            pe.wait_ge(su_w2, 1)
            for f in range(FL):
                last = nc.tensor.transpose(w2t_psum[:, f, :], w2[:, f, :], ident[:, :])
            last.then_inc(su_t1, 1)
            pe.wait_ge(su_c1, 4)
            for f in range(FL):
                last = nc.tensor.matmul(s_psum[:, f, :], mw_t[:, f, :, :].rearrange("p d c -> p (d c)"), cond_t,
                                        start=True, stop=True)
            last.then_inc(su_s, 1)
            pe.wait_ge(su_ss, FL + 1)
            for f in range(FL):
                last = nc.tensor.matmul(d_psum[:, f, :], w2t[0:C, f, :], styles_sq[0:C, f, :], start=True, stop=True)
            last.then_inc(su_d, 1)
            for n in range(6):
                pe.wait_ge(su_wd, 2 * n + 2)
                for k in range(K):
                    last = nc.tensor.transpose(tr[:, k, 0:C], wd[0:C, k, :, :].rearrange("p d c -> p (d c)"),
                                               ident[0:C, 0:C])
                last.then_inc(su_tt, 1)
            for j in range(11):
                src = wbuf[j % 2]
                if j >= 2:
                    pe.wait_ge(su_wc, j - 1)
                dst = ring_f[:, (j % 2) * 1024:(j % 2) * 1024 + 1024].rearrange("p (t n) -> p t n", t=KT)
                by_pos = src[:, :].rearrange("p (b i h) -> p b h i", b=IB, h=2)
                if j < 8:
                    pe.wait_ge(ld_w[j % 2], 16 * (j // 2 + 1))
                    rows = P
                elif j == 8:
                    pe.wait_ge(ld_p0, 32)
                    rows = PROJ0
                elif j == 9:
                    pe.wait_ge(ld_rout, 16)
                    rows = E1
                else:
                    pe.wait_ge(ld_b0, 16 * E0)
                for t in range(KT):
                    if j < 10:
                        last = nc.tensor.transpose(dst[:, t, 0:rows], by_pos[0:rows, t // 2, 1 - t % 2, :],
                                                   ident[0:rows, 0:rows])
                    else:
                        last = nc.tensor.transpose(dst[0:N0, t, :], src[:, t * N0:(t + 1) * N0], ident[:, :])
                last.then_inc(su_wt, 1)
            pe.wait_ge(setup_done, 1)

            def product(dst, w, x, first, last):
                nc.tensor.matmul(dst, w[0], x[0], start=first, stop=False)
                nc.tensor.matmul(dst, w[0], x[1], start=False, stop=False)
                return nc.tensor.matmul(dst, w[1], x[0], start=False, stop=last)

            def tile(g, n):
                return [cw[h][:, g, n, :] for h in range(2)]

            def conv(g, l, s, it):
                if g not in groups(it):
                    return
                n = n_of(g, it)
                if l == 0:
                    pe.wait_ge(p0_ready[g][s], n)
                else:
                    pe.wait_ge(act_done[g][s][l - 1], n * ACT_N[l - 1])
                    pe.wait_ge(lo_done[g][s][l - 1], n * LO_N[l - 1])
                if (g, l) == (0, 1):
                    wait(pe, x1_done, it * 2)
                if (g, l) in ((1, 0), (1, 1), (1, 2)) and 0 in groups(it):
                    other = {0: 1, 1: 2, 2: 3}[l]
                    pe.wait_ge(act_done[0][s][other], (it + 1) * ACT_N[other])
                if (g, l) in ((0, 2), (0, 3)) and 1 in groups(it):
                    pe.wait_ge(act_done[1][s][l - 2], it * ACT_N[l - 2])
                if l == 0:
                    units = [(0, P0, ((0, 0), (1, 1)))]
                elif l == 1:
                    units = [(0, P1, ((2, 0), (3, 1))), (1, P1, ((4, 1), (5, 2)))]
                elif l == 2:
                    units = [(b, P2, ((6, b * H), (7, b * H + 1))) for b in range(2)]
                else:
                    units = [(0, P3, ((8, P3_ODD - 1), (9, 0), (10, P3_ODD), (11, 1)))]
                for bank, src, parts in units:
                    for m, (t, col) in enumerate(parts):
                        last = product(ring[:, s, bank, :], tile(g, t), [src[h][:, s, col:col + H] for h in range(2)],
                                       m == 0, m == len(parts) - 1)
                last.then_inc(conv_done[g][s][l], 1)

            def turn(g, s, it):
                if g not in groups(it):
                    return
                pe.wait_ge(act_done[g][s][3], n_of(g, it))
                if s == 1:
                    pe.wait_ge(yt_hi[g][0], n_of(g, it))
                    pe.wait_ge(yt_lo[g][0], n_of(g, it))
                for b in range(IB):
                    last = nc.tensor.transpose(tr[:, b, :], Y[:, s, b * P:(b + 1) * P], ident[:, :])
                last.then_inc(yt_psum[g][s], 1)

            def over_positions(dst, w, cols):
                for t in range(KT):
                    last = product(dst, [yT[h][:, t, :] for h in range(2)], [w[h][:, t, cols] for h in range(2)],
                                   t == 0, t == KT - 1)
                return last

            def project(g, it):
                if g not in groups(it):
                    return
                for s in range(2):
                    pe.wait_ge(yt_hi[g][s], n_of(g, it))
                    pe.wait_ge(yt_lo[g][s], n_of(g, it))
                if g == 0:
                    last = over_positions(small[:, SM_P0:SM_P0 + PROJ0], w0, slice(0, PROJ0))
                else:
                    last = over_positions(small[:, SM_M1:SM_M1 + MIDS1], w1, slice(L, WC))
                last.then_inc(mids_done[g], 1)

            def turn_gated(g, it):
                if g not in groups(it):
                    return
                pe.wait_ge(gated_done[g], n_of(g, it) * (2 - g))
                col = (SM_GT0, SM_GT1)[g]
                nc.tensor.transpose(small[:, col:col + P], G[g][:, :, :].rearrange("p d n -> p (d n)"), ident[:, :]
                                    ).then_inc(gt_psum[g], 1)

            def lora0(n, it):
                if 0 not in groups(it):
                    return
                pe.wait_ge(gt_hi[0], it + 1)
                pe.wait_ge(gt_lo[0], it + 1)
                for h in range(2):
                    last = nc.tensor.matmul(ring[:, n, 1, :], GT[0][h][:, :], b0s[:, n * H:(n + 1) * H],
                                            start=(h == 0), stop=(h == 1))
                if n == 1:
                    last.then_inc(ffn_done[0], 1)

            def base(n, it):
                if 1 not in groups(it):
                    return
                wait(pe, out_done, it - 1)
                for t in range(KT):
                    product(main[:, n, :], [yT[h][:, t, :] for h in range(2)],
                            [w1[h][:, t, n * H:(n + 1) * H] for h in range(2)], t == 0, False)

            def lora1(it):
                if 1 not in groups(it):
                    return
                pe.wait_ge(gt_hi[1], it)
                pe.wait_ge(gt_lo[1], it)
                for n in range(2):
                    last = product(main[:, n, :], [GT[1][h][:, :] for h in range(2)],
                                   [b1s[h][:, n * H:(n + 1) * H] for h in range(2)], False, True)
                last.then_inc(ffn_done[1], 1)

            def body(it):
                for g, l in ((0, 0), (0, 1), (1, 0), (0, 2), (1, 1), (0, 3)):
                    conv(g, l, 0, it)
                    conv(g, l, 1, it)
                conv(1, 2, 0, it)
                turn(0, 0, it)
                conv(1, 2, 1, it)
                turn(0, 1, it)
                conv(1, 3, 0, it)
                project(0, it)
                conv(1, 3, 1, it)
                turn(1, 0, it)
                turn_gated(0, it)
                lora0(0, it)
                turn(1, 1, it)
                lora0(1, it)
                project(1, it)
                base(0, it)
                turn_gated(1, it)
                base(1, it)
                lora1(it)

            iterations(pe, body)


_INS = ["x", "cond_512", "cond_weights", "cond_biases", "cond_mod_w", "cond_mod_b", "L0_ffn_A", "L0_ffn_B",
        "L0_ffn_Wr", "L1_ffn_base_W", "L1_ffn_router_W", "L1_ffn_lora_A", "L1_ffn_lora_B"]


def kernel(x, cond_512, L0_cond_weights, L0_cond_biases, L0_cond_mod_w, L0_cond_mod_b, L0_ffn_A, L0_ffn_B, L0_ffn_Wr,
           L1_cond_weights, L1_cond_biases, L1_cond_mod_w, L1_cond_mod_b, L1_ffn_base_W, L1_ffn_router_W,
           L1_ffn_lora_A, L1_ffn_lora_B):
    import numpy as np
    import concourse.bacc as bacc
    from concourse.bass_utils import run_bass_kernel_spmd

    values = [x, cond_512,
              np.stack([np.asarray(L0_cond_weights), np.asarray(L1_cond_weights)]),
              np.stack([np.asarray(L0_cond_biases), np.asarray(L1_cond_biases)]).transpose(0, 2, 1),
              np.stack([np.asarray(L0_cond_mod_w), np.asarray(L1_cond_mod_w)]),
              np.stack([np.asarray(L0_cond_mod_b), np.asarray(L1_cond_mod_b)]).transpose(0, 2, 1),
              L0_ffn_A, L0_ffn_B, L0_ffn_Wr, L1_ffn_base_W, L1_ffn_router_W, L1_ffn_lora_A, L1_ffn_lora_B]
    nc = bacc.Bacc("TRN2", target_bir_lowering=False, num_devices=1, dynamic_dma_scratch_size=1024)
    arrays, args = {}, []
    for name, value in zip(_INS, values):
        a = np.ascontiguousarray(value)
        arrays["in_" + name] = a
        args.append(nc.dram_tensor("in_" + name, a.shape, mybir.dt.from_np(a.dtype), kind="ExternalInput").ap())
    out = nc.dram_tensor("out_x", arrays["in_x"].shape, F32, kind="ExternalOutput").ap()
    build(nc, *args, out)
    return run_bass_kernel_spmd(nc, [arrays], core_ids=[0]).results[0]["out_x"]
```

```python
from contextlib import ExitStack

import concourse.bass as bass
from concourse import mybir

F32 = mybir.dt.float32
F32R = mybir.dt.float32r
ALU = mybir.AluOpType
ACT = mybir.ActivationFunctionType
AX_X = mybir.AxisListType.X

P = 128
HALF = 64
PAD_LOGIT = -3.0e38


def build(nc, x, cond_t, conv_t, conv_n1, conv_b, mod_t, mod_b, ffn0_t, lora_b0, ffn1_t, lora_b1, experts, out):
    B, C, L = x.shape
    K = conv_t.shape[3]
    NL = conv_b.shape[2]
    (E0, E1), R = experts, lora_b0.shape[0] // experts[0]
    NPAIR = B // 2
    H = L // 2
    SCALE = 1.0 / float((C * K ** 2) ** 0.5)
    EPS = 1e-8
    N0 = E0 * R
    N1 = E1 * R
    PROJ0 = N0 + E0
    MIDS1 = N1 + E1
    WC = L + MIDS1
    KT = L // P
    IB = KT // 2
    LORA0_SCALE = 16.0 / 4.0
    LORA1_SCALE = 32.0 / 16.0
    assert C == HALF and K == 3 and L == 1024 and N0 == 64 and N1 == 128 and B % 2 == 0 and NPAIR >= 3

    x_rows = x.rearrange("b c t -> (b c) t")
    out_rows = out.rearrange("b c t -> (b c) t")

    with ExitStack() as ctx:
        def sb(name, shape, dt=F32):
            return ctx.enter_context(nc.sbuf_tensor(name, shape, dt))

        def psum(name, shape):
            return ctx.enter_context(nc.psum_tensor(name, shape, F32))

        def sem(name):
            return ctx.enter_context(nc.semaphore(name))

        def sem_gs(name):
            return [[sem(f"{name}_g{g}_s{s}") for s in range(2)] for g in range(2)]

        def sem_gsl(name, layers):
            return [[[sem(f"{name}_g{g}_s{s}_l{l}") for l in range(layers)] for s in range(2)] for g in range(2)]

        TILES = {0: 0, 1: 2, 2: 6, 3: 8}
        NT = 12
        cw = [sb(f"conv_w_{h}", [P, 2, NT, P], F32R) for h in ("hi", "lo")]
        w1 = [sb(f"base_w_{h}", [P, KT, L], F32R) for h in ("hi", "lo")]
        w_mids = [sb("router_lora_a0", [P, KT, 2, PROJ0], F32R), sb("router_lora_a1", [P, KT, 2, MIDS1], F32R)]
        b0s = sb("lora_b0_hi_over_lo", [P, L], F32R)
        b1s = [sb(f"lora_b1_{h}", [P, L], F32R) for h in ("hi", "lo")]

        X2 = sb("x_twice", [P, 2, L + 2])
        P0 = [[sb(f"p0_g{g}_{h}", [P, 2, H + 2], F32R) for h in ("hi", "lo")] for g in range(2)]
        P1 = [sb(f"p1_{h}", [P, 2, H + 2], F32R) for h in ("hi", "lo")]
        P2 = [sb(f"p2_{h}", [P, 2, L + 2], F32R) for h in ("hi", "lo")]
        P3_ODD = H + 3
        P3 = [sb(f"p3_{h}", [P, 2, 2 * P3_ODD], F32R) for h in ("hi", "lo")]
        V = sb("layer_value", [P, 2, L])
        Y = sb("conv_out", [P, 2, H])
        yT = [sb(f"y_t_{h}", [P, KT, P], F32R) for h in ("hi", "lo")]
        XN = sb("x_rows_sb", [P, L])
        X1 = sb("x1_rows", [P, L])
        tab = sb("scales", [P, 2, 8, B])
        T_S0, T_SC0, T_B0, T_SC1, T_B1, T_SC2, T_B2, T_SC3 = range(8)
        act_stage = sb("act_stage", [P, 2, 8, 2])
        pool_stage = sb("pool_stage", [P, 2, 2])
        edge_mask = sb("edge_mask", [P, 2])
        edge_corr = sb("edge_corr", [P, 2, 2, 2])
        bias_nat = sb("conv_bias", [P, 2, NL])
        modb_nat = sb("mod_bias", [P, 2, NL])
        ident = sb("ident", [P, P])
        G = [sb("gated0_twice", [P, 2, N0]), sb("gated1", [P, 1, N1])]
        GT = [[sb(f"gated{g}_t_{h}", [P, P], F32R) for h in ("hi", "lo")] for g in range(2)]
        mids_lo = sb("mids_lo", [P, MIDS1])
        mids = sb("mids", [P, MIDS1])
        top_in = [sb(f"top_in{g}", [P, 16]) for g in range(2)]
        top_q = sb("top_replaced", [P, 16])
        top_max = sb("top_max", [P, 8])
        top_two = [sb(f"top_two{g}", [P, 8]) for g in range(2)]
        neg_max = sb("neg_max", [P, 2])
        gate_e = sb("gate_exp", [P, 2, 8])
        gate_m = sb("gate_masked", [P, 8])
        gate_s = sb("gate_sum", [P, 2])
        gate_r = sb("gate_recip", [P, 2])
        gate = sb("gate", [P, 8])
        wait_taker = sb("wait_taker", [P, 1])

        ring = psum("psum_conv", [P, 2, 2, H])
        main = psum("psum_main", [P, 2, H])
        tr = psum("psum_transposed", [P, 4, P])
        small = psum("psum_small", [P, 512])
        SM_MIDS = (0, 136)
        SM_GT = 0

        ld_small = sem("ld_small")
        ld_wide = [sem(f"ld_wide_{i}") for i in range(2)]
        ident_done = sem("ident_done")
        pads_done = sem("pads_done")
        dve_step = sem("dve_step")
        pool_step = sem("pool_step")
        su_w2 = sem("su_squares")
        su_s = sem("su_styles")
        su_ss = sem("su_styles_squared")
        su_d = sem("su_demod_sums")
        su_v = sem("su_variance")
        su_q = sem("su_sqrt")
        su_tab = sem("su_tables")
        su_wh = sem("su_wide_hi")
        su_wl = sem("su_wide_lo")
        setup_done = sem("setup_done")

        x2_loaded = [sem(f"x2_loaded_s{s}") for s in range(2)]
        x1_doubled = [sem(f"x1_doubled_s{s}") for s in range(2)]
        xn_loaded = sem("xn_loaded")
        p0_part = sem_gs("p0_part")
        p0_ready = sem_gs("p0_ready")
        conv_done = sem_gsl("conv_done", 4)
        value_done = sem_gsl("value_done", 4)
        ends_done = sem_gs("ends_done")
        hi_done = sem_gsl("hi_done", 3)
        hi_bottom_done = sem_gs("layer1_hi_bottom_done")
        lo_done = sem_gsl("lo_done", 3)
        yt_psum = sem_gs("y_transposed")
        yt_hi = sem_gs("yt_hi")
        yt_lo = sem_gs("yt_lo")
        mids_lo_copied = [sem(f"mids_lo_copied_g{g}") for g in range(2)]
        mids_done = [sem(f"mids_done_g{g}") for g in range(2)]
        negmax_done = [sem(f"negmax_done_g{g}") for g in range(2)]
        exp_done = [sem(f"exp_done_g{g}") for g in range(2)]
        gated_done = [sem(f"gated_done_g{g}") for g in range(2)]
        gt_psum = [sem(f"gt_psum_g{g}") for g in range(2)]
        gt_hi = [sem(f"gt_hi_g{g}") for g in range(2)]
        gt_lo = [sem(f"gt_lo_g{g}") for g in range(2)]
        ffn_done = [sem(f"ffn_done_g{g}") for g in range(2)]
        x1_done = [sem(f"x1_done_half{b}") for b in range(2)]
        out_done = sem("out_done")
        out_stored = sem("out_stored")
        x1_kept = sem("x1_kept")
        stage_done = [sem(f"act_stage_done_g{g}") for g in range(2)]
        corr_done = [sem(f"edge_corr_done_g{g}") for g in range(2)]
        gate_step = [sem(f"gate_step_g{g}") for g in range(2)]
        pstage_done = [sem(f"pool_stage_done_g{g}") for g in range(2)]

        Vf = V[:, :, :].rearrange("p s n -> p (s n)")
        Yf = Y[:, :, :].rearrange("p s n -> p (s n)")
        X2f = X2[:, :, :].rearrange("p s n -> p (s n)")
        FL = 2 * NL
        taps = Vf[:, 0:FL * K * C].rearrange("p (f l k c) -> p f l k c", f=2, l=NL, k=K)
        taps1 = Vf[:, FL * K * C:FL * K * C + 2 * K * C].rearrange("p (f k c) -> p f k c", f=2, k=K)
        squares = X2f[:, 0:FL * K * C]
        w2t = Yf.rearrange("p (n d c) -> p n d c", n=FL, d=2)
        mw_t = XN[:, :].rearrange("p (n d c) -> p n d c", n=FL, d=2)
        cond_sb = X1[:, 0:B]
        styles = X2f[:, L + 2:L + 2 + FL * B].rearrange("p (n b) -> p n b", n=FL)
        styles_sq = X2f[:, 0:FL * B].rearrange("p (n b) -> p n b", n=FL)
        dem = Yf[:, 0:FL * B].rearrange("p (n b) -> p n b", n=FL)
        ring_f = ring[:, :, :, :].rearrange("p s b n -> p (s b n)")
        s_psum = ring_f[:, 0:FL * B].rearrange("p (n b) -> p n b", n=FL)
        d_psum = ring_f[:, 1024:1024 + FL * B].rearrange("p (n b) -> p n b", n=FL)
        quad = Yf[:, 0:8 * P].rearrange("p (f t n) -> p f t n", f=2, t=4)
        comb = X2f[:, 0:12 * C].rearrange("p (f n c) -> p f n c", f=2, n=6)
        wide_in = [XN[:, :], X1[:, :]]

        UP = {(-1, 0): (0, 1, 3), (0, 0): (3, 3, 1), (1, 0): (1, 0, 0),
              (-1, 1): (0, 0, 1), (0, 1): (1, 3, 3), (1, 1): (3, 1, 0)}
        UP_KEYS = list(UP)
        DOWN = {-2: (1, 0, 0), -1: (3, 1, 0), 0: (3, 3, 1), 1: (1, 3, 3), 2: (0, 1, 3), 3: (0, 0, 1)}
        DOWN_KEYS = list(DOWN)

        def fixed_quads():
            a = {(0, 0): None, (1, 0): 0, (0, 1): 0, (1, 1): 1}
            b = {(0, 0): 1, (1, 0): 2, (0, 1): 2, (1, 1): None}
            return [a, b]

        def up_quads():
            k = UP_KEYS.index
            return [{(0, 0): k((-1, 1)), (0, 1): k((-1, 0)), (1, 0): None, (1, 1): None},
                    {(0, 0): k((1, 1)), (0, 1): k((1, 0)), (1, 0): k((0, 1)), (1, 1): k((0, 0))},
                    {(0, 0): k((0, 1)), (0, 1): k((0, 0)), (1, 0): k((-1, 1)), (1, 1): k((-1, 0))},
                    {(0, 0): None, (0, 1): None, (1, 0): k((1, 1)), (1, 1): k((1, 0))}]

        def down_quads():
            res = []
            for j in range(4):
                d = {}
                for kh in range(2):
                    for mh in range(2):
                        pos = 2 * (j - 1) + (1 - kh)
                        h = pos - 2 * (1 - mh)
                        d[(kh, mh)] = DOWN_KEYS.index(h) if h in DOWN else None
                res.append(d)
            return res

        def n_of(g, it):
            return it + 1 if g == 0 else it

        def wait(eng, s, count):
            if isinstance(count, int) and count <= 0:
                return
            eng.wait_ge(s, count)

        def groups(it):
            if isinstance(it, int) and it == 0:
                return (0,)
            if isinstance(it, int) and it >= NPAIR:
                return (1,) if it == NPAIR else ()
            return (0, 1)

        def iterations(eng, body):
            body(0)
            body(1)
            with eng.Fori(2, NPAIR - 1) as it:
                body(it)
            body(NPAIR - 1)
            body(NPAIR)

        LO_N = (1, 2, 1)
        GATE_STEPS = (10, 13)
        N_PADS = 19

        def p2_view(h, s, half):
            rows = slice(half * C, half * C + C)
            return P2[h][rows, s, 1 - half:L + 1 - half].rearrange("p (m e) -> p e m", e=2)

        def p3_view(h, s):
            return P3[h][:, s, :].rearrange("p (e j) -> p e j", e=2)[:, :, 0:H]

        def wide_part(j, h):
            buf = wide_in[j % 2]
            if j == 0:
                n = KT * PROJ0
                return (w_mids[0][:, :, h, :], buf[:, 0:n].rearrange("p (t n) -> p t n", t=KT),
                        ffn0_t.rearrange("t p n -> p t n"))
            if j == 1:
                return b0s[h * N0:(h + 1) * N0, :], buf[0:N0, :], lora_b0
            if j == 2:
                return b1s[h][:, :], buf, lora_b1
            if j < 3 + KT:
                return w1[h][:, j - 3, :], buf, ffn1_t[j - 3, :, 0:L]
            a, b = (L, L + N1) if j == 3 + KT else (L + N1, WC)
            return (w_mids[1][:, :, h, a - L:b - L], buf[:, 0:KT * (b - a)].rearrange("p (t n) -> p t n", t=KT),
                    ffn1_t[:, :, a:b].rearrange("t p n -> p t n"))

        WIDE = 3 + KT + 2
        EARLY = 8

        block = ctx.enter_context(nc.Block())

        @block.sync
        def _(sp):
            sp.dma_start(cond_sb, cond_t).then_inc(ld_small, 16)
            for half in range(2):
                rows = slice(half * C, half * C + C)
                sp.dma_start(mw_t[:, :, half, :], mod_t.rearrange("f l s c -> s (f l) c")).then_inc(ld_small, 16)
                sp.dma_start(Vf[rows, 0:FL * K * C], conv_t.rearrange("c f l k o -> c (f l k o)")
                             ).then_inc(ld_small, 16)
                sp.dma_start(Vf[rows, FL * K * C:FL * K * C + 2 * K * C],
                             conv_n1.rearrange("c f k i -> c (f k i)")).then_inc(ld_small, 16)
                sp.dma_start(bias_nat[rows, :, :], conv_b.rearrange("f c l -> c f l")).then_inc(ld_small, 16)
                sp.dma_start(modb_nat[rows, :, :], mod_b.rearrange("f c l -> c f l")).then_inc(ld_small, 16)
            sp.wait_ge(su_s, 1)

            def load_wide(j):
                _, buf, src = wide_part(j, 0)
                if j >= 2:
                    sp.wait_ge(su_wl, j - 1)
                sp.dma_start(buf, src).then_inc(ld_wide[j % 2], 16)

            for j in range(EARLY + 2):
                load_wide(j)
            sp.wait_ge(setup_done, 1)

            def load_doubled(it):
                if 0 not in groups(it):
                    return
                for s in range(2):
                    if isinstance(it, int) and it == 1:
                        sp.wait_ge(p0_ready[0][s], 1)
                    else:
                        wait(sp, p0_ready[1][s], it - 1)
                    src = x_rows[bass.ds(it * P + s * C, C), :]
                    sp.dma_start(X2[0:C, s, 1:L + 1], src).then_inc(x2_loaded[s], 16)
                    sp.dma_start(X2[C:P, s, 0:L], src).then_inc(x2_loaded[s], 16)

            def load_rows(it):
                if 0 not in groups(it):
                    return
                wait(sp, x1_kept, it * 32)
                sp.dma_start(XN[:, :], x_rows[bass.ds(it * P, P), :]).then_inc(xn_loaded, 16)

            load_doubled(0)
            for j in range(EARLY + 2, WIDE):
                load_wide(j)
            sp.wait_ge(su_wl, WIDE)
            load_rows(0)

            def body(it):
                load_doubled(it + 1)
                if 0 in groups(it):
                    if 0 in groups(it + 1):
                        for s in range(2):
                            sp.wait_ge(p0_ready[0][s], it + 2)
                    for b in range(2):
                        sp.wait_ge(x1_done[b], it + 1)
                    for s in range(2):
                        src = XN[s * C:(s + 1) * C, :]
                        sp.dma_start(X2[0:C, s, 1:L + 1], src).then_inc(x1_doubled[s], 16)
                        sp.dma_start(X2[C:P, s, 0:L], src).then_inc(x1_doubled[s], 16)
                if 1 in groups(it):
                    sp.wait_ge(out_done, it)
                    sp.dma_start(out_rows[bass.ds((it - 1) * P, P), :], Yf).then_inc(out_stored, 16)
                if 0 in groups(it):
                    for s in range(2):
                        rows = slice(s * C, (s + 1) * C)
                        sp.dma_start(X1[rows, :], XN[rows, :]).then_inc(x1_kept, 16)
                    for s in range(2):
                        sp.wait_ge(x1_doubled[s], (it + 1) * 32)
                    load_rows(it + 1)

            iterations(sp, body)
            sp.wait_ge(out_stored, 16 * NPAIR)

        @block.gpsimd
        def _(pool):
            nc.gpsimd.memset(ident[:, :], 0.0).then_inc(pool_step, 1)
            pool.wait_ge(pool_step, 1)
            nc.gpsimd.affine_select(out=ident[:, :], in_=ident[:, :], compare_op=ALU.not_equal, fill=1.0,
                                    base=0, pattern=[[-1, P]], channel_multiplier=1).then_inc(ident_done, 1)
            pads = [(P1[h][:, :, c:c + 1].bitcast(F32), 0.0) for h in range(2) for c in (0, H + 1)]
            pads += [(P2[h][rows, :, c:c + 1].bitcast(F32), 0.0) for h in range(2)
                     for rows, c in ((slice(0, C), 0), (slice(C, P), L))]
            pads += [(P3[h][:, :, c:c + 1].bitcast(F32), 0.0) for h in range(2) for c in (H, P3_ODD - 1)]
            pads += [(edge_mask[:, :], -0.125)]
            pads += [(top_in[0][:, :], PAD_LOGIT), (top_two[0][:, :], PAD_LOGIT),
                     (top_in[1][:, :], -1.0), (top_two[1][:, :], -1.0)]
            pads += [(edge_mask[0:C, 0:1], 0.0), (edge_mask[C:P, 1:2], 0.0)]
            assert len(pads) == N_PADS
            for n, (ap, value) in enumerate(pads):
                nc.gpsimd.memset(ap, value).then_inc(pads_done, 1)
                pool.wait_ge(pads_done, n + 1)
            pool.wait_ge(setup_done, 1)
            for s in range(2):
                nc.gpsimd.memset(X2[0:C, s, 0:1], 0.0).then_inc(pool_step, 1)
                pool.wait_ge(pool_step, 2 + 2 * s)
                nc.gpsimd.memset(X2[C:P, s, L:L + 1], 0.0).then_inc(pool_step, 1)
                pool.wait_ge(pool_step, 3 + 2 * s)

            def split(g, s, n):
                src = X2[:, s, 0:L + 1:2]
                style = pool_stage[:, g, s:s + 1].broadcast_to([P, H + 1])
                hi = P0[g][0][:, s, 0:H + 1]
                nc.gpsimd.tensor_tensor(hi, src, style, ALU.mult).then_inc(p0_part[g][s], 1)
                pool.wait_ge(p0_part[g][s], n * 2 - 1)
                nc.gpsimd.tensor_tensor(src, src, style, ALU.mult).then_inc(p0_part[g][s], 1)
                pool.wait_ge(p0_part[g][s], n * 2)
                nc.gpsimd.tensor_tensor(P0[g][1][:, s, 0:H + 1], src, hi.bitcast(F32), ALU.subtract
                                        ).then_inc(p0_ready[g][s], 1)

            def stage(g, pair, count):
                nc.gpsimd.tensor_copy(pool_stage[:, g, :], tab[:, g, T_S0, bass.ds(pair * 2, 2)]
                                      ).then_inc(pstage_done[g], 1)
                pool.wait_ge(pstage_done[g], count)

            def split0(it):
                stage(0, it, it + 1)
                for s in range(2):
                    pool.wait_ge(x2_loaded[s], (it + 1) * 32)
                    wait(pool, conv_done[0][s][0], it)
                    split(0, s, it + 1)

            def split1(it):
                stage(1, it - 1, it)
                for s in range(2):
                    pool.wait_ge(x1_doubled[s], it * 32)
                    wait(pool, conv_done[1][s][0], it - 1)
                    split(1, s, it)

            split0(0)
            split0(1)
            split1(1)
            with pool.Fori(2, NPAIR) as it:
                split0(it)
                split1(it)
            split1(NPAIR)

        @block.scalar
        def _(act):
            act.wait_ge(su_v, 1)
            nc.scalar.activation(dem, dem, ACT.Sqrt).then_inc(su_q, 1)

            def wide_hi(j):
                dst, src, _ = wide_part(j, 0)
                act.wait_ge(ld_wide[j % 2], 16 * (j // 2 + 1))
                nc.scalar.copy(dst, src).then_inc(su_wh, 1)

            for j in range(EARLY):
                wide_hi(j)
            act.wait_ge(setup_done, 1)

            def stage(g, it):
                if g not in groups(it):
                    return
                pair = it if g == 0 else it - 1
                nc.scalar.copy(act_stage[:, g, :, :], tab[:, g, :, bass.ds(pair * 2, 2)]).then_inc(stage_done[g], 1)
                act.wait_ge(stage_done[g], n_of(g, it))
                for s in range(2):
                    nc.scalar.activation(edge_corr[:, g, s, :], edge_mask[:, :], ACT.Copy,
                                         scale=act_stage[:, g, T_B1, s:s + 1]).then_inc(corr_done[g], 1)

            def evacuate(g, l, s, it):
                if g not in groups(it):
                    return
                n = n_of(g, it)
                scale = act_stage[:, g, (T_SC0, T_SC1, T_SC2, T_SC3)[l], s:s + 1]
                bias = act_stage[:, g, (T_B0, T_B1, T_B2)[l], s:s + 1] if l < 3 else bias_nat[:, g, 3:4]
                done = value_done[g][s][l]
                act.wait_ge(conv_done[g][s][l], n)
                if (g, l) == (1, 0) and 0 in groups(it):
                    act.wait_ge(lo_done[0][s][1], (it + 1) * LO_N[1])
                if (g, l) == (0, 2) and 1 in groups(it):
                    act.wait_ge(lo_done[1][s][0], it * LO_N[0])
                if (g, l) == (1, 1) and 0 in groups(it):
                    act.wait_ge(lo_done[0][s][2], (it + 1) * LO_N[2])
                if l == 0:
                    nc.scalar.activation(V[:, s, 0:H], ring[:, s, 0, :], ACT.Identity, bias=bias, scale=scale
                                         ).then_inc(done, 1)
                elif l == 1:
                    nc.scalar.activation(V[:, s, :].rearrange("p (e m) -> p e m", e=2), ring[:, s, :, :],
                                         ACT.Identity, bias=bias, scale=scale).then_inc(done, 1)
                    act.wait_ge(done, n)
                    act.wait_ge(corr_done[g], n * 2)
                    for e in range(2):
                        end = V[:, s, e * (L - 1):e * (L - 1) + 1]
                        nc.scalar.activation(end, end, ACT.Identity, bias=edge_corr[:, g, s, e:e + 1]
                                             ).then_inc(ends_done[g][s], 1)
                    act.wait_ge(ends_done[g][s], n * 2)
                    nc.scalar.copy(p2_view(0, s, 0), V[0:C, s, :].rearrange("p (e m) -> p e m", e=2)
                                   ).then_inc(hi_done[g][s][l], 1)
                elif l == 2:
                    src = ring[:, s, :, :].rearrange("p b n -> p (b n)").rearrange("p (j e) -> p e j", e=2)
                    nc.scalar.activation(V[:, s, :].rearrange("p (e j) -> p e j", e=2), src, ACT.Identity,
                                         bias=bias, scale=scale).then_inc(done, 1)
                else:
                    if g == 0 or (isinstance(it, int) and it == NPAIR):
                        wait(act, out_stored, (it - 1) * 16)
                    nc.scalar.activation(Y[:, s, :], ring[:, s, 0, :], ACT.Identity, bias=bias, scale=scale
                                         ).then_inc(done, 1)

            def turned_hi(g, s, it):
                if g not in groups(it):
                    return
                act.wait_ge(yt_psum[g][s], n_of(g, it))
                nc.scalar.copy(yT[0][:, :, s * C:(s + 1) * C], tr[:, :, :].rearrange("p b (h c) -> p (b h) c", h=2)
                               ).then_inc(yt_hi[g][s], 1)

            def mids_second(g, it):
                if g not in groups(it):
                    return
                n = (PROJ0, MIDS1)[g]
                act.wait_ge(mids_done[g], n_of(g, it))
                if g == 1 and 0 in groups(it):
                    act.wait_ge(gated_done[0], (it + 1) * 2)
                col = SM_MIDS[g] + n
                nc.scalar.copy(mids_lo[:, 0:n], small[:, col:col + n]).then_inc(mids_lo_copied[g], 1)

            def gate_exp(g, it):
                if g not in groups(it):
                    return
                act.wait_ge(negmax_done[g], n_of(g, it))
                nm, ne = ((N0, E0), (N1, E1))[g]
                nc.scalar.activation(gate_e[:, g, 0:ne], mids[:, nm:nm + ne], ACT.Exp, bias=neg_max[:, g:g + 1]
                                     ).then_inc(exp_done[g], 1)

            def gated_hi(g, it):
                if g not in groups(it):
                    return
                act.wait_ge(gt_psum[g], n_of(g, it))
                nc.scalar.copy(GT[g][0][:, :], small[:, SM_GT:SM_GT + P]).then_inc(gt_hi[g], 1)

            stage(0, 0)
            for l in range(2):
                evacuate(0, l, 0, 0)
                evacuate(0, l, 1, 0)

            def body(it):
                stage(1, it)
                evacuate(1, 0, 0, it)
                evacuate(1, 0, 1, it)
                evacuate(0, 2, 0, it)
                evacuate(0, 2, 1, it)
                if isinstance(it, int) and it == 0:
                    for j in range(EARLY, WIDE):
                        wide_hi(j)
                evacuate(1, 1, 0, it)
                evacuate(1, 1, 1, it)
                evacuate(0, 3, 0, it)
                evacuate(0, 3, 1, it)
                evacuate(1, 2, 0, it)
                turned_hi(0, 0, it)
                evacuate(1, 2, 1, it)
                turned_hi(0, 1, it)
                stage(0, it + 1)
                evacuate(1, 3, 0, it)
                mids_second(0, it)
                gate_exp(0, it)
                evacuate(1, 3, 1, it)
                turned_hi(1, 0, it)
                evacuate(0, 0, 0, it + 1)
                gated_hi(0, it)
                turned_hi(1, 1, it)
                evacuate(0, 0, 1, it + 1)
                mids_second(1, it)
                gate_exp(1, it)
                evacuate(0, 1, 0, it + 1)
                gated_hi(1, it)
                evacuate(0, 1, 1, it + 1)

            iterations(act, body)

        @block.vector
        def _(dve):
            chain = [0]

            def link(ins):
                chain[0] += 1
                ins.then_inc(dve_step, 1)
                dve.wait_ge(dve_step, chain[0])

            dve.wait_ge(ld_small, 16 * 11)
            link(nc.vector.tensor_tensor(squares, Vf[:, 0:FL * K * C], Vf[:, 0:FL * K * C], ALU.mult))
            for d in range(2):
                nc.vector.tensor_reduce(w2t[:, :, d, :], squares.rearrange("p (n k c) -> p n c k", n=FL, k=K), AX_X,
                                        ALU.add).then_inc(su_w2, 1)
            dve.wait_ge(su_s, 1)
            dve.wait_ge(su_w2, 2)
            for n in range(FL):
                nc.vector.tensor_scalar(styles[:, n, :], s_psum[:, n, :], modb_nat[:, n // NL, n % NL:n % NL + 1],
                                        None, ALU.add).then_inc(su_ss, 1)
            dve.wait_ge(su_ss, FL)
            nc.vector.tensor_tensor(styles_sq, styles, styles, ALU.mult).then_inc(su_ss, 1)
            dve.wait_ge(su_d, 1)
            nc.vector.tensor_scalar(dem, d_psum, SCALE * SCALE, EPS, ALU.mult, ALU.add).then_inc(su_v, 1)
            dve.wait_ge(su_q, 1)
            link(nc.vector.reciprocal(dem, dem))
            for f in range(2):
                b = NL * f
                nc.vector.tensor_copy(tab[:, f, T_S0, :], styles[:, b, :]).then_inc(dve_step, 1)
                for dst, v, w, factor in ((T_SC0, dem[:, b, :], dem[:, b + 1, :], SCALE),
                                          (T_SC1, styles[:, b + 1, :], styles[:, b + 2, :], SCALE),
                                          (T_SC2, dem[:, b + 2, :], styles[:, b + 3, :], SCALE)):
                    nc.vector.scalar_tensor_tensor(out=tab[:, f, dst, :], in0=v, scalar=factor, in1=w,
                                                   op0=ALU.mult, op1=ALU.mult).then_inc(dve_step, 1)
                for dst, v, l, factor in ((T_B0, dem[:, b + 1, :], 0, 1.0), (T_B1, styles[:, b + 2, :], 1, 2.0),
                                          (T_B2, styles[:, b + 3, :], 2, 1.0)):
                    nc.vector.tensor_scalar(tab[:, f, dst, :], v, bias_nat[:, f, l:l + 1], factor,
                                            ALU.mult, ALU.mult).then_inc(dve_step, 1)
                nc.vector.tensor_scalar(tab[:, f, T_SC3, :], dem[:, b + 3, :], SCALE, None, ALU.mult
                                        ).then_inc(dve_step, 1)
            chain[0] += 16
            dve.wait_ge(dve_step, chain[0])
            nc.vector.memset(top_q[:, :], 0.0).then_inc(su_tab, 1)

            def settle(steps):
                chain[0] += steps
                dve.wait_ge(dve_step, chain[0])

            def wide_lo(j):
                dve.wait_ge(su_wh, j + 1)
                hi, src, _ = wide_part(j, 0)
                nc.vector.tensor_tensor(wide_part(j, 1)[0], src, hi.bitcast(F32), ALU.subtract).then_inc(su_wl, 1)

            for l in range(NL):
                wide_lo(2 * l)
                wide_lo(2 * l + 1)
                src = taps1 if l == 1 else taps[:, :, l, :, :]
                if l in (0, 2):
                    quads = fixed_quads()
                    made = src
                else:
                    weights, norm = (UP, 0.25) if l == 1 else (DOWN, 0.125)
                    some = [[(k, c * norm) for k, c in enumerate(w) if c] for w in weights.values()]
                    for n, w in enumerate(some):
                        nc.vector.tensor_scalar(comb[:, :, n, :], src[:, :, w[0][0], :], w[0][1], None, ALU.mult
                                                ).then_inc(dve_step, 1)
                    settle(len(some))
                    for m in (1, 2):
                        more = [n for n, w in enumerate(some) if len(w) > m]
                        for n in more:
                            nc.vector.scalar_tensor_tensor(out=comb[:, :, n, :], in0=src[:, :, some[n][m][0], :],
                                                           scalar=some[n][m][1], in1=comb[:, :, n, :],
                                                           op0=ALU.mult, op1=ALU.add).then_inc(dve_step, 1)
                        settle(len(more))
                    quads = up_quads() if l == 1 else down_quads()
                    made = comb
                steps = 0
                for t, tile in enumerate(quads):
                    for (kh, mh), n in tile.items():
                        rows = slice(kh * C, kh * C + C)
                        dst = quad[rows, :, t, mh * C:mh * C + C]
                        if n is None:
                            nc.vector.memset(dst, 0.0).then_inc(dve_step, 1)
                        else:
                            nc.vector.tensor_copy(dst, made[rows, :, n, :]).then_inc(dve_step, 1)
                        steps += 1
                settle(steps)
                nt = len(quads)
                hi = cw[0][:, :, TILES[l]:TILES[l] + nt, :]
                link(nc.vector.tensor_copy(hi, quad[:, :, 0:nt, :]))
                link(nc.vector.tensor_tensor(cw[1][:, :, TILES[l]:TILES[l] + nt, :], quad[:, :, 0:nt, :],
                                             hi.bitcast(F32), ALU.subtract))

            assert EARLY == 2 * NL
            dve.wait_ge(su_wl, EARLY)
            dve.wait_ge(pads_done, N_PADS)
            nc.vector.memset(top_q[:, :], 0.0).then_inc(setup_done, 1)

            def low_part(g, l, s, it):
                if g not in groups(it):
                    return
                n = n_of(g, it)
                hi_sem, lo_sem = hi_done[g][s][l], lo_done[g][s][l]
                if l == 0:
                    value, hi, lo = V[:, s, 0:H], P1[0][:, s, 1:H + 1], P1[1][:, s, 1:H + 1]
                elif l == 2:
                    value, hi, lo = V[:, s, :].rearrange("p (e j) -> p e j", e=2), p3_view(0, s), p3_view(1, s)
                if l == 1:
                    dve.wait_ge(ends_done[g][s], n * 2)
                    bottom, top = (V[rows, s, :].rearrange("p (e m) -> p e m", e=2) for rows in (slice(C, P),
                                                                                                 slice(0, C)))
                    nc.vector.tensor_copy(p2_view(0, s, 1), bottom).then_inc(hi_bottom_done[g][s], 1)
                    dve.wait_ge(hi_bottom_done[g][s], n)
                    nc.vector.tensor_tensor(p2_view(1, s, 1), bottom, p2_view(0, s, 1).bitcast(F32), ALU.subtract
                                            ).then_inc(lo_sem, 1)
                    dve.wait_ge(hi_sem, n)
                    nc.vector.tensor_tensor(p2_view(1, s, 0), top, p2_view(0, s, 0).bitcast(F32), ALU.subtract
                                            ).then_inc(lo_sem, 1)
                else:
                    dve.wait_ge(value_done[g][s][l], n)
                    nc.vector.tensor_copy(hi, value).then_inc(hi_sem, 1)
                    dve.wait_ge(hi_sem, n)
                    nc.vector.tensor_tensor(lo, value, hi.bitcast(F32), ALU.subtract).then_inc(lo_sem, 1)

            def turned_lo(g, s, it):
                if g not in groups(it):
                    return
                dve.wait_ge(yt_hi[g][s], n_of(g, it))
                cols = slice(s * C, (s + 1) * C)
                nc.vector.tensor_tensor(yT[1][:, :, cols], tr[:, :, :].rearrange("p b (h c) -> p (b h) c", h=2),
                                        yT[0][:, :, cols].bitcast(F32), ALU.subtract).then_inc(yt_lo[g][s], 1)

            def gating(g, it):
                if g not in groups(it):
                    return
                n = n_of(g, it)
                count = [0]

                def step(ins):
                    count[0] += 1
                    ins.then_inc(gate_step[g], 1)
                    dve.wait_ge(gate_step[g], (n - 1) * GATE_STEPS[g] + count[0])

                def settle():
                    nc.vector.memset(wait_taker[:, :], 0.0)

                dve.wait_ge(mids_lo_copied[g], n)
                col = SM_MIDS[g]
                ne = (E0, E1)[g]
                nm = (N0, N1)[g]
                step(nc.vector.tensor_tensor(mids[:, 0:nm + ne], small[:, col:col + nm + ne], mids_lo[:, 0:nm + ne],
                                             ALU.add))
                logits = mids[:, nm:nm + ne]
                e = gate_e[:, g, 0:ne]
                if g == 0:
                    step(nc.vector.tensor_copy(top_in[0][:, 0:ne], logits))
                    settle()
                    step(nc.vector.max(top_max[:, :], top_in[0][:, :]))
                    nc.vector.tensor_scalar(neg_max[:, 0:1], top_max[:, 0:1], -1.0, None, ALU.mult
                                            ).then_inc(negmax_done[0], 1)
                else:
                    step(nc.vector.tensor_reduce(top_max[:, 0:1], logits, AX_X, ALU.max))
                    nc.vector.tensor_scalar(neg_max[:, 1:2], top_max[:, 0:1], -1.0, None, ALU.mult
                                            ).then_inc(negmax_done[1], 1)
                    dve.wait_ge(exp_done[1], n)
                    step(nc.vector.tensor_reduce(gate_s[:, 1:2], e, AX_X, ALU.add))
                    step(nc.vector.reciprocal(gate_r[:, 1:2], gate_s[:, 1:2]))
                    step(nc.vector.tensor_scalar(top_in[1][:, 0:ne], e, gate_r[:, 1:2], None, ALU.mult))
                    settle()
                    step(nc.vector.max(top_max[:, :], top_in[1][:, :]))
                step(nc.vector.tensor_copy(top_two[g][:, 0:2], top_max[:, 0:2]))
                settle()
                step(nc.vector.match_replace(out=top_q[:, :], in_to_replace=top_two[g][:, :],
                                             in_values=top_in[g][:, :], imm_value=3.0e38))
                step(nc.vector.tensor_tensor(gate_m[:, 0:ne], top_q[:, 0:ne], top_in[g][:, 0:ne], ALU.not_equal))
                if g == 0:
                    dve.wait_ge(exp_done[0], n)
                    step(nc.vector.tensor_tensor(gate[:, 0:ne], gate_m[:, 0:ne], e, ALU.mult))
                else:
                    step(nc.vector.tensor_tensor(gate[:, 0:ne], gate_m[:, 0:ne], top_in[1][:, 0:ne], ALU.mult))
                step(nc.vector.tensor_reduce(gate_s[:, g:g + 1], gate[:, 0:ne], AX_X, ALU.add))
                step(nc.vector.reciprocal(gate_r[:, g:g + 1], gate_s[:, g:g + 1]))
                step(nc.vector.tensor_scalar(gate[:, 0:ne], gate[:, 0:ne], gate_r[:, g:g + 1],
                                             (LORA0_SCALE, LORA1_SCALE)[g], ALU.mult, ALU.mult))
                for d in range(2 - g):
                    nc.vector.tensor_tensor(G[g][:, d, :].rearrange("p (e r) -> p e r", e=ne),
                                            mids[:, 0:nm].rearrange("p (e r) -> p e r", e=ne),
                                            gate[:, 0:ne, None].broadcast_to([P, ne, R]), ALU.mult
                                            ).then_inc(gated_done[g], 1)
                assert count[0] == GATE_STEPS[g]

            def gated_lo(g, it):
                if g not in groups(it):
                    return
                dve.wait_ge(gt_hi[g], n_of(g, it))
                nc.vector.tensor_tensor(GT[g][1][:, :], small[:, SM_GT:SM_GT + P], GT[g][0][:, :].bitcast(F32),
                                        ALU.subtract).then_inc(gt_lo[g], 1)

            def add_out(it):
                if 1 not in groups(it):
                    return
                dve.wait_ge(ffn_done[1], it)
                dve.wait_ge(x1_kept, it * 32)
                nc.vector.tensor_tensor(Y[:, :, :], X1[:, :].rearrange("p (b n) -> p b n", b=2), main[:, :, :],
                                        ALU.add).then_inc(out_done, 1)

            def add_x1(it):
                if 0 not in groups(it):
                    return
                dve.wait_ge(ffn_done[0], it + 1)
                dve.wait_ge(xn_loaded, (it + 1) * 16)
                for b in range(2):
                    cols = slice(b * H, (b + 1) * H)
                    nc.vector.tensor_tensor(XN[:, cols], XN[:, cols], ring[:, b, 1, :], ALU.add
                                            ).then_inc(x1_done[b], 1)

            for l in range(2):
                low_part(0, l, 0, 0)
                low_part(0, l, 1, 0)

            def body(it):
                low_part(1, 0, 0, it)
                low_part(1, 0, 1, it)
                low_part(0, 2, 0, it)
                low_part(0, 2, 1, it)
                if isinstance(it, int) and it == 0:
                    for j in range(EARLY, WIDE):
                        wide_lo(j)
                low_part(1, 1, 0, it)
                low_part(1, 1, 1, it)
                low_part(1, 2, 0, it)
                turned_lo(0, 0, it)
                low_part(1, 2, 1, it)
                turned_lo(0, 1, it)
                gating(0, it)
                turned_lo(1, 0, it)
                low_part(0, 0, 0, it + 1)
                gated_lo(0, it)
                turned_lo(1, 1, it)
                low_part(0, 0, 1, it + 1)
                add_x1(it)
                gating(1, it)
                low_part(0, 1, 0, it + 1)
                gated_lo(1, it)
                low_part(0, 1, 1, it + 1)
                add_out(it)

            iterations(dve, body)

        @block.tensor
        def _(pe):
            pe.wait_ge(ld_small, 16 * 11)
            for n in range(FL):
                last = nc.tensor.matmul(s_psum[:, n, :], mw_t[:, n, :, :].rearrange("p d c -> p (d c)"), cond_sb,
                                        start=True, stop=True)
            last.then_inc(su_s, 1)
            pe.wait_ge(su_ss, FL + 1)
            for n in range(FL):
                last = nc.tensor.matmul(d_psum[:, n, :], w2t[0:C, n, :, :].rearrange("p d c -> p (d c)"),
                                        styles_sq[0:C, n, :], start=True, stop=True)
            last.then_inc(su_d, 1)
            pe.wait_ge(ident_done, 1)
            pe.wait_ge(setup_done, 1)

            def product(dst, w, x, first, last):
                nc.tensor.matmul(dst, w[0], x[0], start=first, stop=False)
                nc.tensor.matmul(dst, w[0], x[1], start=False, stop=False)
                return nc.tensor.matmul(dst, w[1], x[0], start=False, stop=last)

            def tile(g, n):
                return [cw[h][:, g, n, :] for h in range(2)]

            def conv(g, l, s, it):
                if g not in groups(it):
                    return
                n = n_of(g, it)
                if l == 0:
                    pe.wait_ge(p0_ready[g][s], n)
                else:
                    pe.wait_ge(hi_done[g][s][l - 1], n)
                    if l == 2:
                        pe.wait_ge(hi_bottom_done[g][s], n)
                    pe.wait_ge(lo_done[g][s][l - 1], n * LO_N[l - 1])
                if (g, l) == (0, 1):
                    wait(pe, x1_done[s], it)
                if g == 1 and l < 3 and 0 in groups(it):
                    pe.wait_ge(value_done[0][s][l + 1], it + 1)
                if g == 0 and l >= 2 and 1 in groups(it):
                    pe.wait_ge(value_done[1][s][l - 2], it)
                if l == 0:
                    units = [(0, P0[g], ((0, 0), (1, 1)))]
                elif l == 1:
                    units = [(0, P1, ((2, 0), (3, 1))), (1, P1, ((4, 1), (5, 2)))]
                elif l == 2:
                    units = [(b, P2, ((6, b * H), (7, b * H + 1))) for b in range(2)]
                else:
                    units = [(0, P3, ((8, P3_ODD - 1), (9, 0), (10, P3_ODD), (11, 1)))]
                for bank, src, parts in units:
                    for m, (t, col) in enumerate(parts):
                        last = product(ring[:, s, bank, :], tile(g, t), [src[h][:, s, col:col + H] for h in range(2)],
                                       m == 0, m == len(parts) - 1)
                last.then_inc(conv_done[g][s][l], 1)

            def turn(g, s, it):
                if g not in groups(it):
                    return
                pe.wait_ge(value_done[g][s][3], n_of(g, it))
                if s == 1:
                    pe.wait_ge(yt_hi[g][0], n_of(g, it))
                    pe.wait_ge(yt_lo[g][0], n_of(g, it))
                for b in range(IB):
                    last = nc.tensor.transpose(tr[:, b, :], Y[:, s, b * P:(b + 1) * P], ident[:, :])
                last.then_inc(yt_psum[g][s], 1)

            def project(g, it):
                if g not in groups(it):
                    return
                for s in range(2):
                    pe.wait_ge(yt_hi[g][s], n_of(g, it))
                    pe.wait_ge(yt_lo[g][s], n_of(g, it))
                if g == 1 and isinstance(it, int) and it == 1:
                    pe.wait_ge(su_wl, WIDE)
                n, col = (PROJ0, MIDS1)[g], SM_MIDS[g]
                w = w_mids[g]
                for t in range(KT):
                    both = w[:, t, :, :].rearrange("p h n -> p (h n)")
                    last = nc.tensor.matmul(small[:, col:col + 2 * n], yT[0][:, t, :], both,
                                            start=(t == 0), stop=False)
                    last = nc.tensor.matmul(small[:, col:col + n], yT[1][:, t, :], w[:, t, 0, :],
                                            start=False, stop=(t == KT - 1))
                last.then_inc(mids_done[g], 1)

            def turn_gated(g, it):
                if g not in groups(it):
                    return
                pe.wait_ge(gated_done[g], n_of(g, it) * (2 - g))
                nc.tensor.transpose(small[:, SM_GT:SM_GT + P], G[g][:, :, :].rearrange("p d n -> p (d n)"), ident[:, :]
                                    ).then_inc(gt_psum[g], 1)

            def lora0(n, it):
                if 0 not in groups(it):
                    return
                pe.wait_ge(gt_hi[0], it + 1)
                pe.wait_ge(gt_lo[0], it + 1)
                for h in range(2):
                    last = nc.tensor.matmul(ring[:, n, 1, :], GT[0][h][:, :], b0s[:, n * H:(n + 1) * H],
                                            start=(h == 0), stop=(h == 1))
                if n == 1:
                    last.then_inc(ffn_done[0], 1)

            def base(n, it):
                if 1 not in groups(it):
                    return
                wait(pe, out_done, it - 1)
                for t in range(KT):
                    product(main[:, n, :], [yT[h][:, t, :] for h in range(2)],
                            [w1[h][:, t, n * H:(n + 1) * H] for h in range(2)], t == 0, False)

            def lora1(it):
                if 1 not in groups(it):
                    return
                pe.wait_ge(gt_hi[1], it)
                pe.wait_ge(gt_lo[1], it)
                for n in range(2):
                    last = product(main[:, n, :], [GT[1][h][:, :] for h in range(2)],
                                   [b1s[h][:, n * H:(n + 1) * H] for h in range(2)], False, True)
                last.then_inc(ffn_done[1], 1)

            for l in range(2):
                conv(0, l, 0, 0)
                conv(0, l, 1, 0)

            def body(it):
                for g, l in ((1, 0), (0, 2), (1, 1), (0, 3)):
                    conv(g, l, 0, it)
                    conv(g, l, 1, it)
                conv(1, 2, 0, it)
                turn(0, 0, it)
                conv(1, 2, 1, it)
                turn(0, 1, it)
                conv(1, 3, 0, it)
                project(0, it)
                conv(1, 3, 1, it)
                turn(1, 0, it)
                conv(0, 0, 0, it + 1)
                turn_gated(0, it)
                turn(1, 1, it)
                conv(0, 0, 1, it + 1)
                lora0(0, it)
                lora0(1, it)
                project(1, it)
                base(0, it)
                conv(0, 1, 0, it + 1)
                turn_gated(1, it)
                conv(0, 1, 1, it + 1)
                base(1, it)
                lora1(it)

            iterations(pe, body)


_INS = ["x", "cond_t", "conv_t", "conv_n1", "conv_b", "mod_t", "mod_b", "ffn0_t", "lora_b0", "ffn1_t", "lora_b1"]


def layouts(x, cond, conv_w, conv_b, mod_w, mod_b, A0, B0, Wr0, base_w, rout_w, A1, B1):
    import numpy as np

    x, cond, A0, B0, Wr0, base_w, rout_w, A1, B1 = (np.asarray(a) for a in (x, cond, A0, B0, Wr0, base_w, rout_w,
                                                                            A1, B1))
    conv_w, conv_b, mod_w, mod_b = (np.stack([np.asarray(a) for a in v]) for v in (conv_w, conv_b, mod_w, mod_b))
    L = x.shape[2]

    def by_position(a):
        return a.reshape(L // 256, 128, 2, -1)[:, :, ::-1].transpose(0, 2, 1, 3).reshape(L // 128, 128, -1)

    return [x, cond.T, conv_w.transpose(3, 0, 1, 4, 2), conv_w[:, 1].transpose(1, 0, 3, 2), conv_b.transpose(0, 2, 1),
            mod_w.transpose(0, 1, 3, 2), mod_b.transpose(0, 2, 1),
            by_position(np.concatenate([A0.reshape(-1, L).T, Wr0.T], axis=1)),
            B0.transpose(0, 2, 1).reshape(-1, L),
            by_position(np.concatenate([base_w.T, A1.transpose(1, 0, 2).reshape(L, -1), rout_w.T], axis=1)),
            B1.reshape(-1, L)]


def kernel(x, cond_512, L0_cond_weights, L0_cond_biases, L0_cond_mod_w, L0_cond_mod_b, L0_ffn_A, L0_ffn_B, L0_ffn_Wr,
           L1_cond_weights, L1_cond_biases, L1_cond_mod_w, L1_cond_mod_b, L1_ffn_base_W, L1_ffn_router_W,
           L1_ffn_lora_A, L1_ffn_lora_B):
    import numpy as np
    import concourse.bacc as bacc
    from concourse.bass_utils import run_bass_kernel_spmd

    values = layouts(x, cond_512, (L0_cond_weights, L1_cond_weights), (L0_cond_biases, L1_cond_biases),
                     (L0_cond_mod_w, L1_cond_mod_w), (L0_cond_mod_b, L1_cond_mod_b), L0_ffn_A, L0_ffn_B, L0_ffn_Wr,
                     L1_ffn_base_W, L1_ffn_router_W, L1_ffn_lora_A, L1_ffn_lora_B)
    nc = bacc.Bacc("TRN2", target_bir_lowering=False, num_devices=1, dynamic_dma_scratch_size=1024)
    arrays, args = {}, []
    for name, value in zip(_INS, values):
        a = np.ascontiguousarray(value)
        arrays["in_" + name] = a
        args.append(nc.dram_tensor("in_" + name, a.shape, mybir.dt.from_np(a.dtype), kind="ExternalInput").ap())
    out = nc.dram_tensor("out_x", arrays["in_x"].shape, F32, kind="ExternalOutput").ap()
    experts = (L0_ffn_A.shape[0], L1_ffn_lora_A.shape[0])
    build(nc, *args, experts, out)
    return run_bass_kernel_spmd(nc, [arrays], core_ids=[0]).results[0]["out_x"]
```

```python
from contextlib import ExitStack

import concourse.bass as bass
from concourse import mybir

F32 = mybir.dt.float32
F32R = mybir.dt.float32r
ALU = mybir.AluOpType
ACT = mybir.ActivationFunctionType
AX_X = mybir.AxisListType.X

P = 128
HALF = 64
PAD_LOGIT = -3.0e38


def build(nc, x, cond_t, conv_t, conv_b, mod_t, mod_b, ffn0_t, lora_b0, ffn1_t, lora_b1, experts, out):
    B, C, L = x.shape
    K = conv_t.shape[3]
    NL = conv_b.shape[2]
    (E0, E1), R = experts, lora_b0.shape[0] // experts[0]
    NPAIR = B // 2
    H = L // 2
    SCALE = 1.0 / float((C * K ** 2) ** 0.5)
    EPS = 1e-8
    N0 = E0 * R
    N1 = E1 * R
    PROJ0 = N0 + E0
    MIDS1 = N1 + E1
    WC = L + MIDS1
    KT = L // P
    IB = KT // 2
    LORA0_SCALE = 16.0 / 4.0
    LORA1_SCALE = 32.0 / 16.0
    assert C == HALF and K == 3 and L == 1024 and N0 == 64 and N1 == 128 and B % 2 == 0 and NPAIR >= 3

    x_rows = x.rearrange("b c t -> (b c) t")
    out_rows = out.rearrange("b c t -> (b c) t")

    with ExitStack() as ctx:
        def sb(name, shape, dt=F32):
            return ctx.enter_context(nc.sbuf_tensor(name, shape, dt))

        def psum(name, shape):
            return ctx.enter_context(nc.psum_tensor(name, shape, F32))

        def sem(name):
            return ctx.enter_context(nc.semaphore(name))

        def sem_gs(name):
            return [[sem(f"{name}_g{g}_s{s}") for s in range(2)] for g in range(2)]

        def sem_gsl(name, layers):
            return [[[sem(f"{name}_g{g}_s{s}_l{l}") for l in range(layers)] for s in range(2)] for g in range(2)]

        TILES = {0: 0, 1: 2, 3: 6}
        NT = 10
        cw = [sb(f"conv_w_{h}", [P, 2, NT, P], F32R) for h in ("hi", "lo")]
        R2 = sb("layer2_w", [P, 2, 2, P])
        CV = sb("tiles_value", [P, 3 * 2 * P])
        CT = [sb(f"tiles_{h}", [P, 3 * 2 * P], F32R) for h in ("hi", "lo")]
        w1 = [sb(f"base_w_{h}", [P, KT, L], F32R) for h in ("hi", "lo")]
        w_mids = [sb("router_lora_a0", [P, KT, 2, PROJ0], F32R), sb("router_lora_a1", [P, KT, 2, MIDS1], F32R)]
        b0s = sb("lora_b0_hi_over_lo", [P, L], F32R)
        b1s = [sb(f"lora_b1_{h}", [P, L], F32R) for h in ("hi", "lo")]

        X2 = sb("x_twice", [P, 2, L + 2])
        P0 = [[sb(f"p0_g{g}_{h}", [P, 2, H + 2], F32R) for h in ("hi", "lo")] for g in range(2)]
        P1 = [sb(f"p1_{h}", [P, 2, H + 2], F32R) for h in ("hi", "lo")]
        PS = [sb(f"p_shifted_{h}", [P, 2, H + 2], F32R) for h in ("hi", "lo")]
        P3_ODD = H + 3
        P3 = [sb(f"p3_{h}", [P, 2, 2 * P3_ODD], F32R) for h in ("hi", "lo")]
        V = sb("layer_value", [P, 2, 2, H + 1])
        Y = sb("conv_out", [P, 2, H])
        yT = [sb(f"y_t_{h}", [P, KT, P], F32R) for h in ("hi", "lo")]
        XN = sb("x_rows_sb", [P, L])
        X1 = sb("x1_rows", [P, L])
        NTAB = 10
        tab = sb("scales", [P, 2, NTAB, B])
        T_S0, T_SC0, T_B0, T_SC1, T_SC2, T_SC3, T_BI, T_AB, T_C0, T_C1 = range(NTAB)
        act_stage = sb("act_stage", [P, 2, NTAB, 2])
        pool_stage = sb("pool_stage", [P, 2, 2])
        bias_nat = sb("conv_bias", [P, 2, NL])
        modb_nat = sb("mod_bias", [P, 2, NL])
        ident = sb("ident", [P, P])
        G = [sb("gated0_twice", [P, 2, N0]), sb("gated1", [P, 1, N1])]
        GT = [[sb(f"gated{g}_t_{h}", [P, P], F32R) for h in ("hi", "lo")] for g in range(2)]
        mids_lo = sb("mids_lo", [P, MIDS1])
        mids = sb("mids", [P, MIDS1])
        top_in = [sb(f"top_in{g}", [P, 16]) for g in range(2)]
        top_q = sb("top_replaced", [P, 16])
        top_max = sb("top_max", [P, 8])
        top_two = [sb(f"top_two{g}", [P, 8]) for g in range(2)]
        neg_max = sb("neg_max", [P, 2])
        gate_e = sb("gate_exp", [P, 2, 8])
        gate_m = sb("gate_masked", [P, 8])
        gate_s = sb("gate_sum", [P, 2])
        gate_r = sb("gate_recip", [P, 2])
        gate = sb("gate", [P, 8])
        wait_taker = sb("wait_taker", [P, 1])

        ring = psum("psum_conv", [P, 2, 2, H])
        main = psum("psum_main", [P, 2, H])
        tr = psum("psum_transposed", [P, 4, P])
        small = psum("psum_small", [P, 512])
        SM_MIDS = (0, 136)
        SM_GT = 0
        SM_END = 416

        ld_small = sem("ld_small")
        ld_wide = [sem(f"ld_wide_{i}") for i in range(2)]
        ident_done = sem("ident_done")
        pads_done = sem("pads_done")
        dve_step = sem("dve_step")
        pool_step = sem("pool_step")
        su_w2 = sem("su_squares")
        su_s = sem("su_styles")
        su_ss = sem("su_styles_squared")
        su_d = sem("su_demod_sums")
        su_v = sem("su_variance")
        su_q = sem("su_sqrt")
        su_vec = sem("su_bias_vectors")
        su_bias = sem("su_bias_sums")
        su_wh = sem("su_wide_hi")
        su_wl = sem("su_wide_lo")
        setup_done = sem("setup_done")

        x2_loaded = [sem(f"x2_loaded_s{s}") for s in range(2)]
        x1_doubled = [sem(f"x1_doubled_s{s}") for s in range(2)]
        xn_loaded = sem("xn_loaded")
        p0_part = sem_gs("p0_part")
        p0_ready = sem_gs("p0_ready")
        conv_done = sem_gsl("conv_done", 3)
        ends_psum = sem_gs("y2_ends_psum")
        value_done = sem_gsl("value_done", 3)
        hi_done = sem_gsl("hi_done", 2)
        hi_bottom_done = sem_gs("p3_hi_bottom_done")
        lo_done = sem_gsl("lo_done", 2)
        shifted_hi = sem_gs("shifted_hi")
        shifted_lo = sem_gs("shifted_lo")
        scaled_done = [sem(f"r2_scaled_g{g}") for g in range(2)]
        scaled_hi = [sem(f"r2_scaled_hi_g{g}") for g in range(2)]
        scaled_lo = [sem(f"r2_scaled_lo_g{g}") for g in range(2)]
        part_psum = [[sem(f"tile_part_{k}_g{g}") for k in "ab"] for g in range(2)]
        part_copied = [sem(f"tile_part_a_copied_g{g}") for g in range(2)]
        tile_summed = [sem(f"tile_summed_g{g}") for g in range(2)]
        tile_hi = [sem(f"tile_hi_g{g}") for g in range(2)]
        tile_lo = [sem(f"tile_lo_g{g}") for g in range(2)]
        yt_psum = sem_gs("y_transposed")
        yt_hi = sem_gs("yt_hi")
        yt_lo = sem_gs("yt_lo")
        mids_lo_copied = [sem(f"mids_lo_copied_g{g}") for g in range(2)]
        mids_done = [sem(f"mids_done_g{g}") for g in range(2)]
        negmax_done = [sem(f"negmax_done_g{g}") for g in range(2)]
        exp_done = [sem(f"exp_done_g{g}") for g in range(2)]
        gated_done = [sem(f"gated_done_g{g}") for g in range(2)]
        gt_psum = [sem(f"gt_psum_g{g}") for g in range(2)]
        gt_hi = [sem(f"gt_hi_g{g}") for g in range(2)]
        gt_lo = [sem(f"gt_lo_g{g}") for g in range(2)]
        ffn_done = [sem(f"ffn_done_g{g}") for g in range(2)]
        x1_done = [sem(f"x1_done_half{b}") for b in range(2)]
        out_done = sem("out_done")
        out_stored = sem("out_stored")
        x1_kept = sem("x1_kept")
        stage_done = [sem(f"act_stage_done_g{g}") for g in range(2)]
        gate_step = [sem(f"gate_step_g{g}") for g in range(2)]
        pstage_done = [sem(f"pool_stage_done_g{g}") for g in range(2)]

        Vf = V[:, :, :, :].rearrange("p s v n -> p (s v n)")
        Yf = Y[:, :, :].rearrange("p s n -> p (s n)")
        X2f = X2[:, :, :].rearrange("p s n -> p (s n)")
        FL = 2 * NL
        taps = Vf[:, 0:FL * K * C].rearrange("p (f l k c) -> p f l k c", f=2, l=NL, k=K)
        squares = X2f[:, 0:FL * K * C]
        w2t = Yf.rearrange("p (n d c) -> p n d c", n=FL, d=2)
        mw_t = XN[:, :].rearrange("p (n d c) -> p n d c", n=FL, d=2)
        cond_sb = X1[:, 0:B]
        styles = X2f[:, L + 2:L + 2 + FL * B].rearrange("p (n b) -> p n b", n=FL)
        styles_sq = X2f[:, 0:FL * B].rearrange("p (n b) -> p n b", n=FL)
        dem = Yf[:, 0:FL * B].rearrange("p (n b) -> p n b", n=FL)
        ring_f = ring[:, :, :, :].rearrange("p s b n -> p (s b n)")
        s_psum = ring_f[:, 0:FL * B].rearrange("p (n b) -> p n b", n=FL)
        d_psum = ring_f[:, 1024:1024 + FL * B].rearrange("p (n b) -> p n b", n=FL)
        quad = Yf[:, 0:8 * P].rearrange("p (f t n) -> p f t n", f=2, t=4)
        comb = X2f[:, 0:12 * C].rearrange("p (f n c) -> p f n c", f=2, n=6)
        vec = CV[:, :].rearrange("p (f n b) -> p f n b", f=2, n=3)[:, :, :, 0:B]
        bias_psum = ring_f.rearrange("p (f n b) -> p f n b", f=2, b=P)
        wide_in = [XN[:, :], X1[:, :]]

        UP = {(-1, 0): (0, 1, 3), (0, 0): (3, 3, 1), (1, 0): (1, 0, 0),
              (-1, 1): (0, 0, 1), (0, 1): (1, 3, 3), (1, 1): (3, 1, 0)}
        UP_KEYS = list(UP)
        DOWN = {-2: (1, 0, 0), -1: (3, 1, 0), 0: (3, 3, 1), 1: (1, 3, 3), 2: (0, 1, 3), 3: (0, 0, 1)}
        DOWN_KEYS = list(DOWN)

        def fixed_quads():
            a = {(0, 0): None, (1, 0): 0, (0, 1): 0, (1, 1): 1}
            b = {(0, 0): 1, (1, 0): 2, (0, 1): 2, (1, 1): None}
            return [a, b]

        def adjoint_quads():
            res = []
            for top in (-1, 1):
                for j in (-1, 0):
                    res.append({(kh, mh): UP_KEYS.index((top - mh - j, kh)) if abs(top - mh - j) <= 1 else None
                                for kh in range(2) for mh in range(2)})
            return res

        def layer2_quads():
            a = {(0, 0): 0, (1, 0): 1, (0, 1): None, (1, 1): 0}
            b = {(0, 0): 2, (1, 0): None, (0, 1): 1, (1, 1): 2}
            return [a, b]

        def down_quads():
            res = []
            for j in range(4):
                d = {}
                for kh in range(2):
                    for mh in range(2):
                        pos = 2 * (j - 1) + (1 - kh)
                        h = pos - 2 * (1 - mh)
                        d[(kh, mh)] = DOWN_KEYS.index(h) if h in DOWN else None
                res.append(d)
            return res

        def n_of(g, it):
            return it + 1 if g == 0 else it

        def wait(eng, s, count):
            if isinstance(count, int) and count <= 0:
                return
            eng.wait_ge(s, count)

        def groups(it):
            if isinstance(it, int) and it == 0:
                return (0,)
            if isinstance(it, int) and it >= NPAIR:
                return (1,) if it == NPAIR else ()
            return (0, 1)

        def iterations(eng, body):
            body(0)
            body(1)
            with eng.Fori(2, NPAIR - 1) as it:
                body(it)
            body(NPAIR - 1)
            body(NPAIR)

        VALUE_N = (1, 6, 1)
        AFTER_ENDS, AFTER_BANK0 = 4, 3
        LO_N = (1, 3)
        GATE_STEPS = (10, 13)
        N_PADS = 16

        def p3_top(h, s):
            return P3[h][0:C, s, 0:2 * (P3_ODD - 1)].rearrange("p (v m) -> p v m", v=2)[:, :, 0:H + 1]

        def p3_bottom(h, s, v):
            a = (P3_ODD, 0)[v]
            return P3[h][C:P, s, a:a + H]

        def wide_part(j, h):
            buf = wide_in[j % 2]
            if j == 0:
                n = KT * PROJ0
                return (w_mids[0][:, :, h, :], buf[:, 0:n].rearrange("p (t n) -> p t n", t=KT),
                        ffn0_t.rearrange("t p n -> p t n"))
            if j == 1:
                return b0s[h * N0:(h + 1) * N0, :], buf[0:N0, :], lora_b0
            if j == 2:
                return b1s[h][:, :], buf, lora_b1
            if j < 3 + KT:
                return w1[h][:, j - 3, :], buf, ffn1_t[j - 3, :, 0:L]
            a, b = (L, L + N1) if j == 3 + KT else (L + N1, WC)
            return (w_mids[1][:, :, h, a - L:b - L], buf[:, 0:KT * (b - a)].rearrange("p (t n) -> p t n", t=KT),
                    ffn1_t[:, :, a:b].rearrange("t p n -> p t n"))

        WIDE = 3 + KT + 2
        EARLY = 8
        assert WIDE == EARLY + 5

        block = ctx.enter_context(nc.Block())

        @block.sync
        def _(sp):
            sp.dma_start(cond_sb, cond_t).then_inc(ld_small, 16)
            for half in range(2):
                rows = slice(half * C, half * C + C)
                sp.dma_start(mw_t[:, :, half, :], mod_t.rearrange("f l s c -> s (f l) c")).then_inc(ld_small, 16)
                sp.dma_start(Vf[rows, 0:FL * K * C], conv_t.rearrange("c f l k o -> c (f l k o)")
                             ).then_inc(ld_small, 16)
                sp.dma_start(bias_nat[rows, :, :], conv_b.rearrange("f c l -> c f l")).then_inc(ld_small, 16)
                sp.dma_start(modb_nat[rows, :, :], mod_b.rearrange("f c l -> c f l")).then_inc(ld_small, 16)
            sp.wait_ge(su_s, 1)

            def load_wide(j):
                _, buf, src = wide_part(j, 0)
                if j >= 2:
                    sp.wait_ge(su_wl, j - 1)
                sp.dma_start(buf, src).then_inc(ld_wide[j % 2], 16)

            for j in range(EARLY + 2):
                load_wide(j)
            sp.wait_ge(setup_done, 1)

            def load_doubled(it):
                if 0 not in groups(it):
                    return
                for s in range(2):
                    if isinstance(it, int) and it == 1:
                        sp.wait_ge(p0_ready[0][s], 1)
                    else:
                        wait(sp, p0_ready[1][s], it - 1)
                    src = x_rows[bass.ds(it * P + s * C, C), :]
                    sp.dma_start(X2[0:C, s, 1:L + 1], src).then_inc(x2_loaded[s], 16)
                    sp.dma_start(X2[C:P, s, 0:L], src).then_inc(x2_loaded[s], 16)

            def load_rows(it):
                if 0 not in groups(it):
                    return
                wait(sp, x1_kept, it * 32)
                sp.dma_start(XN[:, :], x_rows[bass.ds(it * P, P), :]).then_inc(xn_loaded, 16)

            load_doubled(0)
            for j in range(EARLY + 2, WIDE):
                load_wide(j)
            sp.wait_ge(su_wl, WIDE)
            load_rows(0)

            def body(it):
                load_doubled(it + 1)
                if 0 in groups(it):
                    if 0 in groups(it + 1):
                        for s in range(2):
                            sp.wait_ge(p0_ready[0][s], it + 2)
                    for b in range(2):
                        sp.wait_ge(x1_done[b], it + 1)
                    for s in range(2):
                        src = XN[s * C:(s + 1) * C, :]
                        sp.dma_start(X2[0:C, s, 1:L + 1], src).then_inc(x1_doubled[s], 16)
                        sp.dma_start(X2[C:P, s, 0:L], src).then_inc(x1_doubled[s], 16)
                if 1 in groups(it):
                    sp.wait_ge(out_done, it)
                    sp.dma_start(out_rows[bass.ds((it - 1) * P, P), :], Yf).then_inc(out_stored, 16)
                if 0 in groups(it):
                    for s in range(2):
                        rows = slice(s * C, (s + 1) * C)
                        sp.dma_start(X1[rows, :], XN[rows, :]).then_inc(x1_kept, 16)
                    for s in range(2):
                        sp.wait_ge(x1_doubled[s], (it + 1) * 32)
                    load_rows(it + 1)

            iterations(sp, body)
            sp.wait_ge(out_stored, 16 * NPAIR)

        @block.gpsimd
        def _(pool):
            nc.gpsimd.memset(ident[:, :], 0.0).then_inc(pool_step, 1)
            pool.wait_ge(pool_step, 1)
            nc.gpsimd.affine_select(out=ident[:, :], in_=ident[:, :], compare_op=ALU.not_equal, fill=1.0,
                                    base=0, pattern=[[-1, P]], channel_multiplier=1).then_inc(ident_done, 1)
            pads = [(P1[h][:, :, c:c + 1].bitcast(F32), 0.0) for h in range(2) for c in (0, H + 1)]
            pads += [(PS[h][rows, :, c:c + 1].bitcast(F32), 0.0) for h in range(2)
                     for rows, c in ((slice(0, C), H), (slice(C, P), 0))]
            pads += [(P3[h][:, :, c:c + 1].bitcast(F32), 0.0) for h in range(2) for c in (H, P3_ODD - 1)]
            pads += [(top_in[0][:, :], PAD_LOGIT), (top_two[0][:, :], PAD_LOGIT),
                     (top_in[1][:, :], -1.0), (top_two[1][:, :], -1.0)]
            assert len(pads) == N_PADS
            for n, (ap, value) in enumerate(pads):
                nc.gpsimd.memset(ap, value).then_inc(pads_done, 1)
                pool.wait_ge(pads_done, n + 1)

            def wide_lo(j):
                pool.wait_ge(su_wh, j + 1)
                hi, src, _ = wide_part(j, 0)
                nc.gpsimd.tensor_tensor(wide_part(j, 1)[0], src, hi.bitcast(F32), ALU.subtract).then_inc(su_wl, 1)
                pool.wait_ge(su_wl, j + 1)

            for j in range(EARLY):
                wide_lo(j)
            pool.wait_ge(setup_done, 1)
            for s in range(2):
                nc.gpsimd.memset(X2[0:C, s, 0:1], 0.0).then_inc(pool_step, 1)
                pool.wait_ge(pool_step, 2 + 2 * s)
                nc.gpsimd.memset(X2[C:P, s, L:L + 1], 0.0).then_inc(pool_step, 1)
                pool.wait_ge(pool_step, 3 + 2 * s)

            def split(g, s, n):
                src = X2[:, s, 0:L + 1:2]
                style = pool_stage[:, g, s:s + 1].broadcast_to([P, H + 1])
                hi = P0[g][0][:, s, 0:H + 1]
                nc.gpsimd.tensor_tensor(hi, src, style, ALU.mult).then_inc(p0_part[g][s], 1)
                pool.wait_ge(p0_part[g][s], n * 2 - 1)
                nc.gpsimd.tensor_tensor(src, src, style, ALU.mult).then_inc(p0_part[g][s], 1)
                pool.wait_ge(p0_part[g][s], n * 2)
                nc.gpsimd.tensor_tensor(P0[g][1][:, s, 0:H + 1], src, hi.bitcast(F32), ALU.subtract
                                        ).then_inc(p0_ready[g][s], 1)

            def stage(g, pair, count):
                nc.gpsimd.tensor_copy(pool_stage[:, g, :], tab[:, g, T_S0, bass.ds(pair * 2, 2)]
                                      ).then_inc(pstage_done[g], 1)
                pool.wait_ge(pstage_done[g], count)

            def split0(it):
                stage(0, it, it + 1)
                for s in range(2):
                    pool.wait_ge(x2_loaded[s], (it + 1) * 32)
                    wait(pool, conv_done[0][s][0], it)
                    split(0, s, it + 1)

            def split1(it):
                stage(1, it - 1, it)
                for s in range(2):
                    pool.wait_ge(x1_doubled[s], it * 32)
                    wait(pool, conv_done[1][s][0], it - 1)
                    split(1, s, it)

            split0(0)
            for j in range(EARLY, WIDE):
                wide_lo(j)
            split0(1)
            split1(1)
            with pool.Fori(2, NPAIR) as it:
                split0(it)
                split1(it)
            split1(NPAIR)

        @block.scalar
        def _(act):
            act.wait_ge(su_v, 1)
            nc.scalar.activation(dem, dem, ACT.Sqrt).then_inc(su_q, 1)

            def wide_hi(j):
                dst, src, _ = wide_part(j, 0)
                act.wait_ge(ld_wide[j % 2], 16 * (j // 2 + 1))
                nc.scalar.copy(dst, src).then_inc(su_wh, 1)

            for j in range(EARLY):
                wide_hi(j)
            act.wait_ge(setup_done, 1)

            def stage(g, it):
                if g not in groups(it):
                    return
                pair = it if g == 0 else it - 1
                for s in range(2):
                    wait(act, value_done[g][s][2], n_of(g, it) - 1)
                nc.scalar.copy(act_stage[:, g, :, :], tab[:, g, :, bass.ds(pair * 2, 2)]).then_inc(stage_done[g], 1)
                act.wait_ge(stage_done[g], n_of(g, it))

            def value0(g, s, it):
                if g not in groups(it):
                    return
                act.wait_ge(conv_done[g][s][0], n_of(g, it))
                if g == 1 and 0 in groups(it):
                    act.wait_ge(lo_done[0][s][1], (it + 1) * LO_N[1])
                if g == 0:
                    wait(act, lo_done[1][s][1], (it - 1) * LO_N[1])
                scale, bias = (act_stage[:, g, t, s:s + 1] for t in (T_SC0, T_B0))
                nc.scalar.activation(V[:, s, 0, 0:H], ring[:, s, 0, :], ACT.Identity, bias=bias, scale=scale
                                     ).then_inc(value_done[g][s][0], 1)

            def shift_hi(g, s, it):
                if g not in groups(it):
                    return
                act.wait_ge(hi_done[g][s][0], n_of(g, it))
                nc.scalar.copy(PS[0][0:C, s, 0:H], P1[0][C:P, s, 1:H + 1].bitcast(F32)).then_inc(shifted_hi[g][s], 1)
                nc.scalar.copy(PS[0][C:P, s, 1:H + 1], P1[0][0:C, s, 1:H + 1].bitcast(F32)
                               ).then_inc(shifted_hi[g][s], 1)

            def value12(g, s, it):
                if g not in groups(it):
                    return

                def scaled(dst, src, bias, rows):
                    nc.scalar.activation(dst, src, ACT.Identity, bias=act_stage[rows, g, bias, s:s + 1],
                                         scale=act_stage[rows, g, T_SC2, s:s + 1]).then_inc(value_done[g][s][1], 1)

                every, top, bottom = slice(0, P), slice(0, C), slice(C, P)
                act.wait_ge(ends_psum[g][s], n_of(g, it))
                scaled(V[bottom, s, 1, 0:1], small[bottom, SM_END:SM_END + 1], T_AB, bottom)
                scaled(V[top, s, 1, H:H + 1], small[top, SM_END + 1:SM_END + 2], T_AB, top)
                act.wait_ge(conv_done[g][s][1], n_of(g, it) * 2 - 1)
                scaled(V[:, s, 1, 1:H], ring[:, s, 0, 1:H], T_BI, every)
                act.wait_ge(conv_done[g][s][1], n_of(g, it) * 2)
                scaled(V[:, s, 0, 1:H - 1], ring[:, s, 1, 1:H - 1], T_BI, every)
                scaled(V[:, s, 0, 0:1], ring[:, s, 1, 0:1], T_C0, every)
                scaled(V[:, s, 0, H - 1:H], ring[:, s, 1, H - 1:H], T_C1, every)

            def y2_hi_top(g, s, it):
                if g not in groups(it):
                    return
                act.wait_ge(value_done[g][s][1], n_of(g, it) * VALUE_N[1])
                nc.scalar.copy(p3_top(0, s), V[0:C, s, :, :]).then_inc(hi_done[g][s][1], 1)

            def value3(g, s, it):
                if g not in groups(it):
                    return
                act.wait_ge(conv_done[g][s][2], n_of(g, it))
                if g == 0 or (isinstance(it, int) and it == NPAIR):
                    wait(act, out_stored, (it - 1) * 16)
                nc.scalar.activation(Y[:, s, :], ring[:, s, 1, :], ACT.Identity, bias=bias_nat[:, g, 3:4],
                                     scale=act_stage[:, g, T_SC3, s:s + 1]).then_inc(value_done[g][s][2], 1)

            def r2_hi(g, it):
                if g not in groups(it):
                    return
                act.wait_ge(scaled_done[g], n_of(g, it))
                for s in range(2):
                    if g == 1 and 0 in groups(it):
                        act.wait_ge(conv_done[0][s][1], (it + 1) * 2)
                    if g == 0:
                        wait(act, conv_done[1][s][1], (it - 1) * 2)
                nc.scalar.copy(CT[0][:, 0:4 * P], CV[:, 0:4 * P]).then_inc(scaled_hi[g], 1)

            def part_a(g, it):
                if g not in groups(it):
                    return
                act.wait_ge(part_psum[g][0], n_of(g, it))
                nc.scalar.copy(CV[:, 0:4 * P], main[:, 0, :]).then_inc(part_copied[g], 1)
                nc.scalar.copy(CV[:, 4 * P:6 * P].rearrange("p (s n) -> p s n", s=2)[:, :, 0:C],
                               main[:, 0, 0:2 * P].rearrange("p (s n) -> p s n", s=2)[:, :, 0:C]
                               ).then_inc(part_copied[g], 1)

            def tiles_hi(g, it):
                if g not in groups(it):
                    return
                act.wait_ge(tile_summed[g], n_of(g, it) * 2)
                act.wait_ge(part_copied[g], n_of(g, it) * 2)
                nc.scalar.copy(CT[0][:, :], CV[:, :]).then_inc(tile_hi[g], 1)

            def turned_hi(g, s, it):
                if g not in groups(it):
                    return
                act.wait_ge(yt_psum[g][s], n_of(g, it))
                nc.scalar.copy(yT[0][:, :, s * C:(s + 1) * C], tr[:, :, :].rearrange("p b (h c) -> p (b h) c", h=2)
                               ).then_inc(yt_hi[g][s], 1)

            def mids_second(g, it):
                if g not in groups(it):
                    return
                n = (PROJ0, MIDS1)[g]
                act.wait_ge(mids_done[g], n_of(g, it))
                if g == 1 and 0 in groups(it):
                    act.wait_ge(gated_done[0], (it + 1) * 2)
                col = SM_MIDS[g] + n
                nc.scalar.copy(mids_lo[:, 0:n], small[:, col:col + n]).then_inc(mids_lo_copied[g], 1)

            def gate_exp(g, it):
                if g not in groups(it):
                    return
                act.wait_ge(negmax_done[g], n_of(g, it))
                nm, ne = ((N0, E0), (N1, E1))[g]
                nc.scalar.activation(gate_e[:, g, 0:ne], mids[:, nm:nm + ne], ACT.Exp, bias=neg_max[:, g:g + 1]
                                     ).then_inc(exp_done[g], 1)

            def gated_hi(g, it):
                if g not in groups(it):
                    return
                act.wait_ge(gt_psum[g], n_of(g, it))
                nc.scalar.copy(GT[g][0][:, :], small[:, SM_GT:SM_GT + P]).then_inc(gt_hi[g], 1)

            stage(0, 0)
            r2_hi(0, 0)
            part_a(0, 0)
            tiles_hi(0, 0)
            wide_hi(EARLY)
            for s in range(2):
                value0(0, s, 0)
                shift_hi(0, s, 0)
                wide_hi(EARLY + 1 + s)
            for s in range(2):
                value12(0, s, 0)
                y2_hi_top(0, s, 0)
                wide_hi(EARLY + 3 + s)

            def body(it):
                value0(1, 0, it)
                value0(1, 1, it)
                part_a(1, it)
                shift_hi(1, 1, it)
                shift_hi(1, 0, it)
                tiles_hi(1, it)
                value3(0, 0, it)
                value3(0, 1, it)
                stage(0, it + 1)
                turned_hi(0, 0, it)
                value12(1, 0, it)
                turned_hi(0, 1, it)
                y2_hi_top(1, 0, it)
                value12(1, 1, it)
                r2_hi(0, it + 1)
                value0(0, 0, it + 1)
                y2_hi_top(1, 1, it)
                mids_second(0, it)
                shift_hi(0, 0, it + 1)
                gate_exp(0, it)
                part_a(0, it + 1)
                value3(1, 0, it)
                value3(1, 1, it)
                gated_hi(0, it)
                turned_hi(1, 0, it)
                tiles_hi(0, it + 1)
                value0(0, 1, it + 1)
                shift_hi(0, 1, it + 1)
                turned_hi(1, 1, it)
                value12(0, 0, it + 1)
                mids_second(1, it)
                gate_exp(1, it)
                stage(1, it + 1)
                y2_hi_top(0, 0, it + 1)
                value12(0, 1, it + 1)
                r2_hi(1, it + 1)
                gated_hi(1, it)
                y2_hi_top(0, 1, it + 1)
            iterations(act, body)

        @block.vector
        def _(dve):
            chain = [0]

            def link(ins):
                chain[0] += 1
                ins.then_inc(dve_step, 1)
                dve.wait_ge(dve_step, chain[0])

            dve.wait_ge(ld_small, 16 * 9)
            link(nc.vector.tensor_tensor(squares, Vf[:, 0:FL * K * C], Vf[:, 0:FL * K * C], ALU.mult))
            for d in range(2):
                nc.vector.tensor_reduce(w2t[:, :, d, :], squares.rearrange("p (n k c) -> p n c k", n=FL, k=K), AX_X,
                                        ALU.add).then_inc(su_w2, 1)
            dve.wait_ge(su_s, 1)
            dve.wait_ge(su_w2, 2)
            for n in range(FL):
                nc.vector.tensor_scalar(styles[:, n, :], s_psum[:, n, :], modb_nat[:, n // NL, n % NL:n % NL + 1],
                                        None, ALU.add).then_inc(su_ss, 1)
            dve.wait_ge(su_ss, FL)
            nc.vector.tensor_tensor(styles_sq, styles, styles, ALU.mult).then_inc(su_ss, 1)
            dve.wait_ge(su_d, 1)
            nc.vector.tensor_scalar(dem, d_psum, SCALE * SCALE, EPS, ALU.mult, ALU.add).then_inc(su_v, 1)
            dve.wait_ge(su_q, 1)
            link(nc.vector.reciprocal(dem, dem))
            for f in range(2):
                b = NL * f
                nc.vector.tensor_copy(tab[:, f, T_S0, :], styles[:, b, :]).then_inc(dve_step, 1)
                for dst, v, w, factor in ((T_SC0, dem[:, b, :], dem[:, b + 1, :], SCALE),
                                          (T_SC1, styles[:, b + 1, :], styles[:, b + 2, :], SCALE),
                                          (T_SC2, dem[:, b + 2, :], styles[:, b + 3, :], SCALE)):
                    nc.vector.scalar_tensor_tensor(out=tab[:, f, dst, :], in0=v, scalar=factor, in1=w,
                                                   op0=ALU.mult, op1=ALU.mult).then_inc(dve_step, 1)
                for dst, v, l, factor in ((tab[:, f, T_B0, :], dem[:, b + 1, :], 0, 1.0),
                                          (vec[:, f, 0, :], styles[:, b + 2, :], 1, 2.0),
                                          (tab[:, f, T_BI, :], styles[:, b + 3, :], 2, 1.0)):
                    nc.vector.tensor_scalar(dst, v, bias_nat[:, f, l:l + 1], factor,
                                            ALU.mult, ALU.mult).then_inc(dve_step, 1)
                nc.vector.tensor_scalar(tab[:, f, T_SC3, :], dem[:, b + 3, :], SCALE, None, ALU.mult
                                        ).then_inc(dve_step, 1)
            chain[0] += 16
            dve.wait_ge(dve_step, chain[0])
            for n in (1, 2):
                for half in range(2):
                    rows = slice(half * C, half * C + C)
                    nc.vector.tensor_scalar(vec[rows, :, n, :], vec[rows, :, 0, :],
                                            0.875 if half == 2 - n else 1.0, None, ALU.mult).then_inc(su_vec, 1)

            def settle(steps):
                chain[0] += steps
                dve.wait_ge(dve_step, chain[0])

            for l in range(NL):
                src = taps[:, :, l, :, :]
                if l in (0, 2):
                    quads = fixed_quads() if l == 0 else layer2_quads()
                    made = src
                else:
                    weights, norm = (UP, 0.25) if l == 1 else (DOWN, 0.125)
                    some = [[(k, c * norm) for k, c in enumerate(w) if c] for w in weights.values()]
                    for n, w in enumerate(some):
                        nc.vector.tensor_scalar(comb[:, :, n, :], src[:, :, w[0][0], :], w[0][1], None, ALU.mult
                                                ).then_inc(dve_step, 1)
                    settle(len(some))
                    for m in (1, 2):
                        more = [n for n, w in enumerate(some) if len(w) > m]
                        for n in more:
                            nc.vector.scalar_tensor_tensor(out=comb[:, :, n, :], in0=src[:, :, some[n][m][0], :],
                                                           scalar=some[n][m][1], in1=comb[:, :, n, :],
                                                           op0=ALU.mult, op1=ALU.add).then_inc(dve_step, 1)
                        settle(len(more))
                    quads = adjoint_quads() if l == 1 else down_quads()
                    made = comb
                steps = 0
                for t, tile in enumerate(quads):
                    for (kh, mh), n in tile.items():
                        rows = slice(kh * C, kh * C + C)
                        dst = (R2 if l == 2 else quad)[rows, :, t, mh * C:mh * C + C]
                        if n is None:
                            nc.vector.memset(dst, 0.0).then_inc(dve_step, 1)
                        else:
                            nc.vector.tensor_copy(dst, made[rows, :, n, :]).then_inc(dve_step, 1)
                        steps += 1
                settle(steps)
                if l == 2:
                    nc.vector.memset(top_q[:, :], 0.0).then_inc(su_vec, 1)
                    continue
                nt = len(quads)
                hi = cw[0][:, :, TILES[l]:TILES[l] + nt, :]
                link(nc.vector.tensor_copy(hi, quad[:, :, 0:nt, :]))
                link(nc.vector.tensor_tensor(cw[1][:, :, TILES[l]:TILES[l] + nt, :], quad[:, :, 0:nt, :],
                                             hi.bitcast(F32), ALU.subtract))

            dve.wait_ge(su_bias, 1)
            top, bottom = slice(0, C), slice(C, P)
            for f in range(2):
                for t, rows, n in ((T_AB, top, 1), (T_AB, bottom, 2), (T_C0, top, 3), (T_C0, bottom, 0),
                                   (T_C1, top, 0), (T_C1, bottom, 4)):
                    nc.vector.tensor_tensor(tab[rows, f, t, :], bias_psum[rows, f, n, 0:B], tab[rows, f, T_SC2, :],
                                            ALU.mult).then_inc(dve_step, 1)
                nc.vector.tensor_tensor(vec[:, f, 0, :], bias_psum[:, f, 0, 0:B], tab[:, f, T_SC2, :],
                                        ALU.mult).then_inc(dve_step, 1)
            settle(14)
            for f in range(2):
                for t in (T_AB, T_C0, T_C1):
                    nc.vector.tensor_tensor(tab[:, f, t, :], tab[:, f, t, :], tab[:, f, T_BI, :], ALU.add
                                            ).then_inc(dve_step, 1)
            settle(6)
            for f in range(2):
                nc.vector.tensor_tensor(tab[:, f, T_BI, :], tab[:, f, T_BI, :], vec[:, f, 0, :], ALU.add
                                        ).then_inc(dve_step, 1)
            nc.vector.memset(V[0:C, :, 0, H:H + 1], 0.0).then_inc(dve_step, 1)
            nc.vector.memset(V[0:C, :, 1, 0:1], 0.0).then_inc(dve_step, 1)
            settle(4)
            dve.wait_ge(su_wl, EARLY)
            dve.wait_ge(pads_done, N_PADS)
            nc.vector.memset(top_q[:, :], 0.0).then_inc(setup_done, 1)

            def split0(g, s, it):
                if g not in groups(it):
                    return
                n = n_of(g, it)
                value, hi, lo = V[:, s, 0, 0:H], P1[0][:, s, 1:H + 1], P1[1][:, s, 1:H + 1]
                dve.wait_ge(value_done[g][s][0], n)
                nc.vector.tensor_copy(hi, value).then_inc(hi_done[g][s][0], 1)
                dve.wait_ge(hi_done[g][s][0], n)
                nc.vector.tensor_tensor(lo, value, hi.bitcast(F32), ALU.subtract).then_inc(lo_done[g][s][0], 1)

            def shift_lo(g, s, it):
                if g not in groups(it):
                    return
                dve.wait_ge(lo_done[g][s][0], n_of(g, it))
                nc.vector.tensor_copy(PS[1][0:C, s, 0:H], P1[1][C:P, s, 1:H + 1].bitcast(F32)
                                      ).then_inc(shifted_lo[g][s], 1)
                nc.vector.tensor_copy(PS[1][C:P, s, 1:H + 1], P1[1][0:C, s, 1:H + 1].bitcast(F32)
                                      ).then_inc(shifted_lo[g][s], 1)

            def split12(g, s, it):
                if g not in groups(it):
                    return
                n = n_of(g, it)
                dve.wait_ge(value_done[g][s][1], n * VALUE_N[1])
                for v in range(2):
                    nc.vector.tensor_copy(p3_bottom(0, s, v), V[C:P, s, v, 0:H]).then_inc(hi_bottom_done[g][s], 1)
                for v in range(2):
                    dve.wait_ge(hi_bottom_done[g][s], n * 2 - 1 + v)
                    nc.vector.tensor_tensor(p3_bottom(1, s, v), V[C:P, s, v, 0:H], p3_bottom(0, s, v).bitcast(F32),
                                            ALU.subtract).then_inc(lo_done[g][s][1], 1)
                dve.wait_ge(hi_done[g][s][1], n)
                nc.vector.tensor_tensor(p3_top(1, s), V[0:C, s, :, :], p3_top(0, s).bitcast(F32), ALU.subtract
                                        ).then_inc(lo_done[g][s][1], 1)

            def scale_r2(g, it):
                if g not in groups(it):
                    return
                dve.wait_ge(stage_done[g], n_of(g, it))
                if g == 1 and 0 in groups(it):
                    dve.wait_ge(tile_lo[0], it + 1)
                if g == 0:
                    wait(dve, tile_lo[1], it - 1)
                nc.vector.tensor_tensor(CV[:, 0:4 * P].rearrange("p (k s n) -> p k s n", k=2, s=2),
                                        R2[:, g, :, None, :].broadcast_to([P, 2, 2, P]),
                                        act_stage[:, g, T_SC1, None, :, None].broadcast_to([P, 2, 2, P]), ALU.mult
                                        ).then_inc(scaled_done[g], 1)

            def r2_lo(g, it):
                if g not in groups(it):
                    return
                dve.wait_ge(scaled_hi[g], n_of(g, it))
                nc.vector.tensor_tensor(CT[1][:, 0:4 * P], CV[:, 0:4 * P], CT[0][:, 0:4 * P].bitcast(F32),
                                        ALU.subtract).then_inc(scaled_lo[g], 1)

            def sum_tiles(g, it):
                if g not in groups(it):
                    return
                dve.wait_ge(part_psum[g][1], n_of(g, it))
                dve.wait_ge(part_copied[g], n_of(g, it) * 2)
                nc.vector.tensor_tensor(CV[:, 0:4 * P], CV[:, 0:4 * P], main[:, 1, :], ALU.add
                                        ).then_inc(tile_summed[g], 1)
                nc.vector.tensor_copy(CV[:, 4 * P:6 * P].rearrange("p (s n) -> p s n", s=2)[:, :, C:P],
                                      main[:, 1, 2 * P:4 * P].rearrange("p (s n) -> p s n", s=2)[:, :, C:P]
                                      ).then_inc(tile_summed[g], 1)

            def tiles_lo(g, it):
                if g not in groups(it):
                    return
                dve.wait_ge(tile_hi[g], n_of(g, it))
                nc.vector.tensor_tensor(CT[1][:, :], CV[:, :], CT[0][:, :].bitcast(F32), ALU.subtract
                                        ).then_inc(tile_lo[g], 1)

            def turned_lo(g, s, it):
                if g not in groups(it):
                    return
                dve.wait_ge(yt_hi[g][s], n_of(g, it))
                cols = slice(s * C, (s + 1) * C)
                nc.vector.tensor_tensor(yT[1][:, :, cols], tr[:, :, :].rearrange("p b (h c) -> p (b h) c", h=2),
                                        yT[0][:, :, cols].bitcast(F32), ALU.subtract).then_inc(yt_lo[g][s], 1)

            def gating(g, it):
                if g not in groups(it):
                    return
                n = n_of(g, it)
                count = [0]

                def step(ins):
                    count[0] += 1
                    ins.then_inc(gate_step[g], 1)
                    dve.wait_ge(gate_step[g], (n - 1) * GATE_STEPS[g] + count[0])

                def settle():
                    nc.vector.memset(wait_taker[:, :], 0.0)

                dve.wait_ge(mids_lo_copied[g], n)
                col = SM_MIDS[g]
                ne = (E0, E1)[g]
                nm = (N0, N1)[g]
                step(nc.vector.tensor_tensor(mids[:, 0:nm + ne], small[:, col:col + nm + ne], mids_lo[:, 0:nm + ne],
                                             ALU.add))
                logits = mids[:, nm:nm + ne]
                e = gate_e[:, g, 0:ne]
                if g == 0:
                    step(nc.vector.tensor_copy(top_in[0][:, 0:ne], logits))
                    settle()
                    step(nc.vector.max(top_max[:, :], top_in[0][:, :]))
                    nc.vector.tensor_scalar(neg_max[:, 0:1], top_max[:, 0:1], -1.0, None, ALU.mult
                                            ).then_inc(negmax_done[0], 1)
                else:
                    step(nc.vector.tensor_reduce(top_max[:, 0:1], logits, AX_X, ALU.max))
                    nc.vector.tensor_scalar(neg_max[:, 1:2], top_max[:, 0:1], -1.0, None, ALU.mult
                                            ).then_inc(negmax_done[1], 1)
                    dve.wait_ge(exp_done[1], n)
                    step(nc.vector.tensor_reduce(gate_s[:, 1:2], e, AX_X, ALU.add))
                    step(nc.vector.reciprocal(gate_r[:, 1:2], gate_s[:, 1:2]))
                    step(nc.vector.tensor_scalar(top_in[1][:, 0:ne], e, gate_r[:, 1:2], None, ALU.mult))
                    settle()
                    step(nc.vector.max(top_max[:, :], top_in[1][:, :]))
                step(nc.vector.tensor_copy(top_two[g][:, 0:2], top_max[:, 0:2]))
                settle()
                step(nc.vector.match_replace(out=top_q[:, :], in_to_replace=top_two[g][:, :],
                                             in_values=top_in[g][:, :], imm_value=3.0e38))
                step(nc.vector.tensor_tensor(gate_m[:, 0:ne], top_q[:, 0:ne], top_in[g][:, 0:ne], ALU.not_equal))
                if g == 0:
                    dve.wait_ge(exp_done[0], n)
                    step(nc.vector.tensor_tensor(gate[:, 0:ne], gate_m[:, 0:ne], e, ALU.mult))
                else:
                    step(nc.vector.tensor_tensor(gate[:, 0:ne], gate_m[:, 0:ne], top_in[1][:, 0:ne], ALU.mult))
                step(nc.vector.tensor_reduce(gate_s[:, g:g + 1], gate[:, 0:ne], AX_X, ALU.add))
                step(nc.vector.reciprocal(gate_r[:, g:g + 1], gate_s[:, g:g + 1]))
                step(nc.vector.tensor_scalar(gate[:, 0:ne], gate[:, 0:ne], gate_r[:, g:g + 1],
                                             (LORA0_SCALE, LORA1_SCALE)[g], ALU.mult, ALU.mult))
                for d in range(2 - g):
                    nc.vector.tensor_tensor(G[g][:, d, :].rearrange("p (e r) -> p e r", e=ne),
                                            mids[:, 0:nm].rearrange("p (e r) -> p e r", e=ne),
                                            gate[:, 0:ne, None].broadcast_to([P, ne, R]), ALU.mult
                                            ).then_inc(gated_done[g], 1)
                assert count[0] == GATE_STEPS[g]

            def gated_lo(g, it):
                if g not in groups(it):
                    return
                dve.wait_ge(gt_hi[g], n_of(g, it))
                nc.vector.tensor_tensor(GT[g][1][:, :], small[:, SM_GT:SM_GT + P], GT[g][0][:, :].bitcast(F32),
                                        ALU.subtract).then_inc(gt_lo[g], 1)

            def add_out(it):
                if 1 not in groups(it):
                    return
                dve.wait_ge(ffn_done[1], it)
                dve.wait_ge(x1_kept, it * 32)
                nc.vector.tensor_tensor(Y[:, :, :], X1[:, :].rearrange("p (b n) -> p b n", b=2), main[:, :, :],
                                        ALU.add).then_inc(out_done, 1)

            def add_x1(it):
                if 0 not in groups(it):
                    return
                dve.wait_ge(ffn_done[0], it + 1)
                dve.wait_ge(xn_loaded, (it + 1) * 16)
                for b in range(2):
                    cols = slice(b * H, (b + 1) * H)
                    nc.vector.tensor_tensor(XN[:, cols], XN[:, cols], ring[:, b, 1, :], ALU.add
                                            ).then_inc(x1_done[b], 1)

            scale_r2(0, 0)
            r2_lo(0, 0)
            sum_tiles(0, 0)
            tiles_lo(0, 0)
            for s in range(2):
                split0(0, s, 0)
                shift_lo(0, s, 0)
            for s in range(2):
                split12(0, s, 0)

            def body(it):
                split0(1, 0, it)
                split0(1, 1, it)
                shift_lo(1, 0, it)
                sum_tiles(1, it)
                shift_lo(1, 1, it)
                tiles_lo(1, it)
                scale_r2(0, it + 1)
                turned_lo(0, 0, it)
                turned_lo(0, 1, it)
                split12(1, 0, it)
                r2_lo(0, it + 1)
                split12(1, 1, it)
                split0(0, 0, it + 1)
                gating(0, it)
                sum_tiles(0, it + 1)
                gated_lo(0, it)
                shift_lo(0, 0, it + 1)
                turned_lo(1, 0, it)
                tiles_lo(0, it + 1)
                split0(0, 1, it + 1)
                add_x1(it)
                turned_lo(1, 1, it)
                shift_lo(0, 1, it + 1)
                gating(1, it)
                scale_r2(1, it + 1)
                split12(0, 0, it + 1)
                r2_lo(1, it + 1)
                gated_lo(1, it)
                split12(0, 1, it + 1)
                add_out(it)
            iterations(dve, body)

        @block.tensor
        def _(pe):
            pe.wait_ge(ld_small, 16 * 9)
            for n in range(FL):
                last = nc.tensor.matmul(s_psum[:, n, :], mw_t[:, n, :, :].rearrange("p d c -> p (d c)"), cond_sb,
                                        start=True, stop=True)
            last.then_inc(su_s, 1)
            pe.wait_ge(su_ss, FL + 1)
            for n in range(FL):
                last = nc.tensor.matmul(d_psum[:, n, :], w2t[0:C, n, :, :].rearrange("p d c -> p (d c)"),
                                        styles_sq[0:C, n, :], start=True, stop=True)
            last.then_inc(su_d, 1)
            pe.wait_ge(su_vec, 5)
            for f in range(2):
                for n, parts in enumerate((((0, 0), (1, 0)), ((0, 1),), ((1, 2),), ((0, 2), (1, 0)),
                                           ((0, 0), (1, 1)))):
                    for m, (k, v) in enumerate(parts):
                        last = nc.tensor.matmul(bias_psum[:, f, n, 0:B], R2[:, f, k, :], vec[:, f, v, :],
                                                start=(m == 0), stop=(m == len(parts) - 1))
            last.then_inc(su_bias, 1)
            pe.wait_ge(ident_done, 1)
            pe.wait_ge(setup_done, 1)

            def product(dst, w, x, first, last):
                nc.tensor.matmul(dst, w[0], x[0], start=first, stop=False)
                nc.tensor.matmul(dst, w[0], x[1], start=False, stop=False)
                return nc.tensor.matmul(dst, w[1], x[0], start=False, stop=last)

            def tile(g, n):
                return [cw[h][:, g, n, :] for h in range(2)]

            def build_tiles(g, it):
                if g not in groups(it):
                    return
                pe.wait_ge(scaled_lo[g], n_of(g, it))
                if g == 1:
                    wait(pe, out_done, it - 1)
                    if 0 in groups(it):
                        pe.wait_ge(tile_summed[0], (it + 1) * 2)
                else:
                    wait(pe, tile_summed[1], (it - 1) * 2)
                for k in range(2):
                    for y in range(2):
                        last = product(main[:, k, y * 2 * P:(y + 1) * 2 * P], tile(g, TILES[1] + 2 * y + k),
                                       [CT[h][:, k * 2 * P:(k + 1) * 2 * P] for h in range(2)], True, True)
                    last.then_inc(part_psum[g][k], 1)

            def chain(dst, g, src, s, parts):
                for m, (t, col) in enumerate(parts):
                    last = product(dst, tile(g, t), [src[h][:, s, col:col + H] for h in range(2)],
                                   m == 0, m == len(parts) - 1)
                return last

            def conv0(g, s, it):
                if g not in groups(it):
                    return
                pe.wait_ge(p0_ready[g][s], n_of(g, it))
                if g == 1 and 0 in groups(it):
                    pe.wait_ge(value_done[0][s][1], (it + 1) * VALUE_N[1] - AFTER_BANK0)
                if g == 0:
                    wait(pe, value_done[1][s][1], (it - 1) * VALUE_N[1] - AFTER_BANK0)
                chain(ring[:, s, 0, :], g, P0[g], s, ((0, 0), (1, 1))).then_inc(conv_done[g][s][0], 1)

            def conv12(g, s, it):
                if g not in groups(it):
                    return
                n = n_of(g, it)
                pe.wait_ge(hi_done[g][s][0], n)
                pe.wait_ge(lo_done[g][s][0], n)
                pe.wait_ge(shifted_hi[g][s], n * 2)
                pe.wait_ge(shifted_lo[g][s], n * 2)
                pe.wait_ge(tile_lo[g], n)

                def sample_tile(y):
                    return [CT[h][:, (2 * y + s) * P:(2 * y + s + 1) * P] for h in range(2)]

                if g == 0 and s == 1:
                    wait(pe, gated_done[1], it - 1)
                if s == 1:
                    pe.wait_ge(value_done[g][0][1], n * VALUE_N[1] - AFTER_ENDS)
                elif g == 1 and 0 in groups(it):
                    pe.wait_ge(value_done[0][1][1], (it + 1) * VALUE_N[1] - AFTER_ENDS)
                product(small[:, SM_END:SM_END + 2], sample_tile(2), [P1[h][:, s, 1:H + 1:H - 1] for h in range(2)],
                        True, True).then_inc(ends_psum[g][s], 1)
                for bank, src in ((0, P1), (1, PS)):
                    if bank == 1 and g == 0:
                        wait(pe, x1_done[s], it)
                    elif bank == 1 and 0 in groups(it):
                        pe.wait_ge(value_done[0][s][2], it + 1)
                    for y in range(2):
                        last = product(ring[:, s, bank, :], sample_tile(y), [src[h][:, s, y:y + H] for h in range(2)],
                                       y == 0, y == 1)
                    last.then_inc(conv_done[g][s][1], 1)

            def conv3(g, s, it):
                if g not in groups(it):
                    return
                n = n_of(g, it)
                pe.wait_ge(hi_done[g][s][1], n)
                pe.wait_ge(hi_bottom_done[g][s], n * 2)
                pe.wait_ge(lo_done[g][s][1], n * LO_N[1])
                t = TILES[3]
                chain(ring[:, s, 1, :], g, P3, s, ((t, P3_ODD - 1), (t + 1, 0), (t + 2, P3_ODD), (t + 3, 1))
                      ).then_inc(conv_done[g][s][2], 1)

            def turn(g, s, it):
                if g not in groups(it):
                    return
                pe.wait_ge(value_done[g][s][2], n_of(g, it))
                if s == 1:
                    pe.wait_ge(yt_hi[g][0], n_of(g, it))
                    pe.wait_ge(yt_lo[g][0], n_of(g, it))
                for b in range(IB):
                    last = nc.tensor.transpose(tr[:, b, :], Y[:, s, b * P:(b + 1) * P], ident[:, :])
                last.then_inc(yt_psum[g][s], 1)

            def project(g, it):
                if g not in groups(it):
                    return
                for s in range(2):
                    pe.wait_ge(yt_hi[g][s], n_of(g, it))
                    pe.wait_ge(yt_lo[g][s], n_of(g, it))
                if g == 0 and 1 in groups(it):
                    pe.wait_ge(value_done[1][1][1], it * VALUE_N[1] - AFTER_ENDS)
                if g == 1 and 0 in groups(it + 1):
                    pe.wait_ge(value_done[0][0][1], (it + 2) * VALUE_N[1] - AFTER_ENDS)
                if g == 1 and isinstance(it, int) and it == 1:
                    pe.wait_ge(su_wl, WIDE)
                n, col = (PROJ0, MIDS1)[g], SM_MIDS[g]
                w = w_mids[g]
                for t in range(KT):
                    both = w[:, t, :, :].rearrange("p h n -> p (h n)")
                    last = nc.tensor.matmul(small[:, col:col + 2 * n], yT[0][:, t, :], both,
                                            start=(t == 0), stop=False)
                    last = nc.tensor.matmul(small[:, col:col + n], yT[1][:, t, :], w[:, t, 0, :],
                                            start=False, stop=(t == KT - 1))
                last.then_inc(mids_done[g], 1)

            def turn_gated(g, it):
                if g not in groups(it):
                    return
                pe.wait_ge(gated_done[g], n_of(g, it) * (2 - g))
                if g == 1 and 0 in groups(it + 1):
                    pe.wait_ge(value_done[0][1][1], (it + 2) * VALUE_N[1] - AFTER_ENDS)
                nc.tensor.transpose(small[:, SM_GT:SM_GT + P], G[g][:, :, :].rearrange("p d n -> p (d n)"), ident[:, :]
                                    ).then_inc(gt_psum[g], 1)

            def lora0(n, it):
                if 0 not in groups(it):
                    return
                pe.wait_ge(gt_hi[0], it + 1)
                pe.wait_ge(gt_lo[0], it + 1)
                if 1 in groups(it):
                    pe.wait_ge(value_done[1][n][2], it)
                for h in range(2):
                    last = nc.tensor.matmul(ring[:, n, 1, :], GT[0][h][:, :], b0s[:, n * H:(n + 1) * H],
                                            start=(h == 0), stop=(h == 1))
                if n == 1:
                    last.then_inc(ffn_done[0], 1)

            def base(n, it):
                if 1 not in groups(it):
                    return
                wait(pe, out_done, it - 1)
                pe.wait_ge(tile_summed[1], it * 2)
                if 0 in groups(it + 1):
                    pe.wait_ge(tile_summed[0], (it + 2) * 2)
                for t in range(KT):
                    product(main[:, n, :], [yT[h][:, t, :] for h in range(2)],
                            [w1[h][:, t, n * H:(n + 1) * H] for h in range(2)], t == 0, False)

            def lora1(it):
                if 1 not in groups(it):
                    return
                pe.wait_ge(gt_hi[1], it)
                pe.wait_ge(gt_lo[1], it)
                for n in range(2):
                    last = product(main[:, n, :], [GT[1][h][:, :] for h in range(2)],
                                   [b1s[h][:, n * H:(n + 1) * H] for h in range(2)], False, True)
                last.then_inc(ffn_done[1], 1)

            build_tiles(0, 0)
            conv0(0, 0, 0)
            conv0(0, 1, 0)
            conv12(0, 0, 0)
            conv12(0, 1, 0)

            def body(it):
                conv0(1, 0, it)
                conv0(1, 1, it)
                build_tiles(1, it)
                conv3(0, 0, it)
                conv3(0, 1, it)
                turn(0, 0, it)
                conv12(1, 0, it)
                turn(0, 1, it)
                conv12(1, 1, it)
                conv0(0, 0, it + 1)
                project(0, it)
                conv3(1, 0, it)
                build_tiles(0, it + 1)
                conv3(1, 1, it)
                turn_gated(0, it)
                turn(1, 0, it)
                conv0(0, 1, it + 1)
                lora0(0, it)
                turn(1, 1, it)
                lora0(1, it)
                conv12(0, 0, it + 1)
                project(1, it)
                base(0, it)
                conv12(0, 1, it + 1)
                turn_gated(1, it)
                base(1, it)
                lora1(it)
            iterations(pe, body)


_INS = ["x", "cond_t", "conv_t", "conv_b", "mod_t", "mod_b", "ffn0_t", "lora_b0", "ffn1_t", "lora_b1"]


def layouts(x, cond, conv_w, conv_b, mod_w, mod_b, A0, B0, Wr0, base_w, rout_w, A1, B1):
    import numpy as np

    x, cond, A0, B0, Wr0, base_w, rout_w, A1, B1 = (np.asarray(a) for a in (x, cond, A0, B0, Wr0, base_w, rout_w,
                                                                            A1, B1))
    conv_w, conv_b, mod_w, mod_b = (np.stack([np.asarray(a) for a in v]) for v in (conv_w, conv_b, mod_w, mod_b))
    L = x.shape[2]

    def by_position(a):
        return a.reshape(L // 256, 128, 2, -1)[:, :, ::-1].transpose(0, 2, 1, 3).reshape(L // 128, 128, -1)

    return [x, cond.T, conv_w.transpose(3, 0, 1, 4, 2), conv_b.transpose(0, 2, 1),
            mod_w.transpose(0, 1, 3, 2), mod_b.transpose(0, 2, 1),
            by_position(np.concatenate([A0.reshape(-1, L).T, Wr0.T], axis=1)),
            B0.transpose(0, 2, 1).reshape(-1, L),
            by_position(np.concatenate([base_w.T, A1.transpose(1, 0, 2).reshape(L, -1), rout_w.T], axis=1)),
            B1.reshape(-1, L)]


def kernel(x, cond_512, L0_cond_weights, L0_cond_biases, L0_cond_mod_w, L0_cond_mod_b, L0_ffn_A, L0_ffn_B, L0_ffn_Wr,
           L1_cond_weights, L1_cond_biases, L1_cond_mod_w, L1_cond_mod_b, L1_ffn_base_W, L1_ffn_router_W,
           L1_ffn_lora_A, L1_ffn_lora_B):
    import numpy as np
    import concourse.bacc as bacc
    from concourse.bass_utils import run_bass_kernel_spmd

    values = layouts(x, cond_512, (L0_cond_weights, L1_cond_weights), (L0_cond_biases, L1_cond_biases),
                     (L0_cond_mod_w, L1_cond_mod_w), (L0_cond_mod_b, L1_cond_mod_b), L0_ffn_A, L0_ffn_B, L0_ffn_Wr,
                     L1_ffn_base_W, L1_ffn_router_W, L1_ffn_lora_A, L1_ffn_lora_B)
    nc = bacc.Bacc("TRN2", target_bir_lowering=False, num_devices=1, dynamic_dma_scratch_size=1024)
    arrays, args = {}, []
    for name, value in zip(_INS, values):
        a = np.ascontiguousarray(value)
        arrays["in_" + name] = a
        args.append(nc.dram_tensor("in_" + name, a.shape, mybir.dt.from_np(a.dtype), kind="ExternalInput").ap())
    out = nc.dram_tensor("out_x", arrays["in_x"].shape, F32, kind="ExternalOutput").ap()
    experts = (L0_ffn_A.shape[0], L1_ffn_lora_A.shape[0])
    build(nc, *args, experts, out)
    return run_bass_kernel_spmd(nc, [arrays], core_ids=[0]).results[0]["out_x"]
```
